# Optimizing a Trainium2 kernel written in Bass

```python
import numpy as np
import jax
import jax.numpy as jnp

def _softmax(x, axis=-1):
    return jax.nn.softmax(x, axis=axis)

def _gelu(x):
    return jax.nn.gelu(x, approximate=True)

def _silu(x):
    return jax.nn.silu(x)

def _sigmoid(x):
    return jax.nn.sigmoid(x)

def _layernorm(x, axis=-1, eps=1e-05):
    m = jnp.mean(x, axis=axis, keepdims=True)
    v = jnp.var(x, axis=axis, keepdims=True)
    return (x - m) / jnp.sqrt(v + eps)

def _scatter_add(tgt, idx, src, axis=0):
    return tgt.at[idx].add(src)

def _segment_sum(src, seg, n):
    return jax.ops.segment_sum(src, seg, n)
kernel_name = 'mk_adaln_ffn_d1_seqx_r8_3a8685'

def setup_inputs(seed: int=0):
    np.random.seed(seed)
    _w = jnp.asarray

    def _rec_inputs():
        import jax
        import jax.numpy as jnp
        _rk = jax.random.key(seed)
        x = -0.000125 + 0.9999 * jax.random.normal(jax.random.fold_in(_rk, 1), (32, 32, 512), jnp.float32)
        _lenS = 32 - jax.random.randint(jax.random.fold_in(_rk, 7), (32,), 0, max(1, 32 // 4) + 1, jnp.int32)
        _lenS2 = 32 - jax.random.randint(jax.random.fold_in(_rk, 8), (32,), 0, max(1, 32 // 4) + 1, jnp.int32)
        itok_B_0_23 = jax.random.randint(jax.random.fold_in(_rk, 11), (32,), 0, 24, jnp.int32)
        return (x, itok_B_0_23)
    x, itok_B_0_23 = _rec_inputs()

    def _L0_cond_setup():
        import jax, jax.numpy as jnp
        import numpy as np
        R = 16
        ALPHA = 32
        SCALING = ALPHA / R
        SLOTS = 32
        IN_F = 512
        OUT_F = 512
        B, T = (8, 128)
        key = jax.random.key(seed)
        k1, k2, k3, k4, k5, k6 = jax.random.split(key, 6)
        x = jax.random.normal(k1, (B, T, IN_F), dtype=jnp.float32)
        adapter_mapping = jax.random.randint(k2, (B,), 0, SLOTS, dtype=jnp.int32)
        W = jax.random.normal(k3, (OUT_F, IN_F), dtype=jnp.float32) * 0.02
        b = jax.random.normal(k4, (OUT_F,), dtype=jnp.float32) * 0.02
        lora_As = jax.random.normal(k5, (SLOTS, IN_F, R), dtype=jnp.float32) * 0.02
        lora_Bs = jax.random.normal(k6, (SLOTS, R, OUT_F), dtype=jnp.float32) * 0.02
        return {'x': x, 'adapter_mapping': adapter_mapping, 'W': W, 'b': b, 'lora_As': lora_As, 'lora_Bs': lora_Bs}
    _L0_cond_all = _L0_cond_setup()
    _L0_cond_in = {k: v for k, v in _L0_cond_all.items() if k in ('W', 'b', 'lora_As', 'lora_Bs')}
    del _L0_cond_all

    def _L0_ffn_setup():
        import jax, jax.numpy as jnp
        import numpy as np
        DIM = 512
        INTER = 128
        E = 16
        GROUPS = 4
        LIM = 2
        K = 2
        SHARED_INTER = 2 * INTER
        SCALE = 1.0
        key = jax.random.key(seed)
        ks = jax.random.split(key, 16)

        def n(k, shape, s=0.02):
            return jax.random.normal(k, shape, jnp.float32) * s
        return {'x': jax.random.normal(ks[0], (1, 256, DIM), jnp.float32), 'router_w': n(ks[1], (DIM, E)), 'router_b': n(ks[2], (E,)), 'router_bias': n(ks[3], (E,), 1.0), 'ew1': n(ks[4], (E, DIM, INTER)), 'eb1': n(ks[5], (E, INTER)), 'ew2': n(ks[6], (E, DIM, INTER)), 'eb2': n(ks[7], (E, INTER)), 'ew3': n(ks[8], (E, INTER, DIM)), 'eb3': n(ks[9], (E, DIM)), 'sw1': n(ks[10], (DIM, SHARED_INTER)), 'sb1': n(ks[11], (SHARED_INTER,)), 'sw2': n(ks[12], (DIM, SHARED_INTER)), 'sb2': n(ks[13], (SHARED_INTER,)), 'sw3': n(ks[14], (SHARED_INTER, DIM)), 'sb3': n(ks[15], (DIM,))}
    _L0_ffn_all = _L0_ffn_setup()
    _L0_ffn_in = {k: v for k, v in _L0_ffn_all.items() if k in ('router_w', 'router_b', 'router_bias', 'ew1', 'eb1', 'ew2', 'eb2', 'ew3', 'eb3', 'sw1', 'sb1', 'sw2', 'sb2', 'sw3', 'sb3')}
    del _L0_ffn_all
    return {'x': x, 'itok_B_0_23': itok_B_0_23, 'L0_cond_W': _L0_cond_in['W'], 'L0_cond_b': _L0_cond_in['b'], 'L0_cond_lora_As': _L0_cond_in['lora_As'], 'L0_cond_lora_Bs': _L0_cond_in['lora_Bs'], 'L0_ffn_router_w': _L0_ffn_in['router_w'], 'L0_ffn_router_b': _L0_ffn_in['router_b'], 'L0_ffn_router_bias': _L0_ffn_in['router_bias'], 'L0_ffn_ew1': _L0_ffn_in['ew1'], 'L0_ffn_eb1': _L0_ffn_in['eb1'], 'L0_ffn_ew2': _L0_ffn_in['ew2'], 'L0_ffn_eb2': _L0_ffn_in['eb2'], 'L0_ffn_ew3': _L0_ffn_in['ew3'], 'L0_ffn_eb3': _L0_ffn_in['eb3'], 'L0_ffn_sw1': _L0_ffn_in['sw1'], 'L0_ffn_sb1': _L0_ffn_in['sb1'], 'L0_ffn_sw2': _L0_ffn_in['sw2'], 'L0_ffn_sb2': _L0_ffn_in['sb2'], 'L0_ffn_sw3': _L0_ffn_in['sw3'], 'L0_ffn_sb3': _L0_ffn_in['sb3']}

def reference(x, itok_B_0_23, L0_cond_W, L0_cond_b, L0_cond_lora_As, L0_cond_lora_Bs, L0_ffn_router_w, L0_ffn_router_b, L0_ffn_router_bias, L0_ffn_ew1, L0_ffn_eb1, L0_ffn_ew2, L0_ffn_eb2, L0_ffn_ew3, L0_ffn_eb3, L0_ffn_sw1, L0_ffn_sb1, L0_ffn_sw2, L0_ffn_sb2, L0_ffn_sw3, L0_ffn_sb3):
    import jax
    import jax.numpy as jnp

    def _L0_cond_ref(x, adapter_mapping, W, b, lora_As, lora_Bs):
        import jax, jax.numpy as jnp
        import numpy as np
        R = 16
        ALPHA = 32
        SCALING = ALPHA / R
        SLOTS = 32
        IN_F = 512
        OUT_F = 512
        B, T = (8, 128)
        base_out = jnp.einsum('bti,oi->bto', x, W) + b
        A = lora_As[adapter_mapping]
        Bm = lora_Bs[adapter_mapping]
        lora_h = jnp.einsum('bti,bir->btr', x, A)
        lora_out = jnp.einsum('btr,bro->bto', lora_h, Bm)
        return base_out + lora_out * SCALING

    def _L0_ffn_ref(x, router_w, router_b, router_bias, ew1, eb1, ew2, eb2, ew3, eb3, sw1, sb1, sw2, sb2, sw3, sb3):
        import jax, jax.numpy as jnp
        import numpy as np
        DIM = 512
        INTER = 128
        E = 16
        GROUPS = 4
        LIM = 2
        K = 2
        SHARED_INTER = 2 * INTER
        SCALE = 1.0
        shape = x.shape
        xt = x.reshape(-1, DIM)
        T = xt.shape[0]
        logits = xt @ router_w + router_b
        scores = jax.nn.softmax(logits.astype(jnp.float32), axis=-1) + router_bias
        g = scores.reshape(T, GROUPS, E // GROUPS)
        _, gidx = jax.lax.top_k(g.max(axis=-1), LIM)
        keep = jnp.zeros((T, GROUPS), bool).at[jnp.arange(T)[:, None], gidx].set(True)
        masked = jnp.where(keep[:, :, None], g, -jnp.inf).reshape(T, E)
        _, idx = jax.lax.top_k(masked, K)
        vals = (jnp.take_along_axis(scores, idx, axis=1) * SCALE).astype(x.dtype)
        gate = jnp.zeros((T, E), x.dtype).at[jnp.arange(T)[:, None], idx].add(vals)

        def step(y, p):
            w1, b1, w2, b2, w3, b3, ge = p
            h = jax.nn.silu(xt @ w1 + b1) * (xt @ w2 + b2)
            return (y + ge[:, None] * (h @ w3 + b3), None)
        y, _ = jax.lax.scan(step, jnp.zeros_like(xt), (ew1, eb1, ew2, eb2, ew3, eb3, gate.T))
        z = jax.nn.silu(xt @ sw1 + sb1) * (xt @ sw2 + sb2) @ sw3 + sb3
        return (y + z).reshape(shape)
    x = x + _L0_ffn_ref(_L0_cond_ref(x, itok_B_0_23, L0_cond_W, L0_cond_b, L0_cond_lora_As, L0_cond_lora_Bs), L0_ffn_router_w, L0_ffn_router_b, L0_ffn_router_bias, L0_ffn_ew1, L0_ffn_eb1, L0_ffn_ew2, L0_ffn_eb2, L0_ffn_ew3, L0_ffn_eb3, L0_ffn_sw1, L0_ffn_sb1, L0_ffn_sw2, L0_ffn_sb2, L0_ffn_sw3, L0_ffn_sb3)
    return x

_drawn_inputs = setup_inputs


def setup_inputs(seed=0):
    import zlib

    import numpy as np

    out = dict(_drawn_inputs(seed))
    spreads = {}
    factors = {'L0_cond_W': 3.676,
     'L0_cond_b': 8.0,
     'L0_cond_lora_As': 8.0,
     'L0_cond_lora_Bs': 8.0,
     'L0_ffn_router_w': 8.0,
     'L0_ffn_router_b': 40.341,
     'L0_ffn_ew1': 4.176,
     'L0_ffn_eb1': 64.0,
     'L0_ffn_ew2': 4.131,
     'L0_ffn_eb2': 64.0,
     'L0_ffn_ew3': 4.107,
     'L0_ffn_sw1': 8.0,
     'L0_ffn_sb1': 53.812,
     'L0_ffn_sw2': 8.0,
     'L0_ffn_sb2': 52.941,
     'L0_ffn_sw3': 8.0,
     'L0_ffn_sb3': 22.776,
     'L0_ffn_eb3': 8.0}
    for name, (base, spread) in spreads.items():
        noise = np.random.default_rng([zlib.crc32(name.encode()), seed]).standard_normal(out[name].shape)
        drawn = base * np.exp(spread * noise) if base else spread * noise
        out[name] = jnp.asarray(drawn.astype(out[name].dtype))
    for name, factor in factors.items():
        out[name] = (out[name] * factor).astype(out[name].dtype)
    return out
```

```python
from contextlib import ExitStack

import concourse.bass as bass
from concourse import mybir

F32 = mybir.dt.float32
I32 = mybir.dt.int32
ALU = mybir.AluOpType
ACT = mybir.ActivationFunctionType
AX = mybir.AxisListType

P = 128
SEQS, SEQ_LEN, DIM = 32, 32, 512
T = SEQS * SEQ_LEN
TILES = T // P
KC = DIM // P
SLOTS, RANK = 32, 16
LORA_SCALE = 32 / RANK
SEQ_PER_TILE = P // SEQ_LEN
LR = SEQ_PER_TILE * RANK
GROUPS_L = SEQS * RANK // P
E, INTER, SHARED = 16, 128, 256
GROUPS, PER_GROUP, LIM, K = 4, 4, 2, 2
BLOCKS = (K * T + E * (P - 1)) // P
BPAD = 32
W12 = KC * 2 * INTER
IC = SHARED // P
HALF = T // 2
XCHUNKS = 4
CH = T // XCHUNKS
BIG = 3.0e38
UNROLL = 4


def program(nc, x, xT, seq_slot, condWT, cond_b, lora, router_w, router_b, router_bias,
            w12, b12, w3, b3s, sw12, sb12, sw3, out):
    xt_rows = nc.dram_tensor("xt_rows", (T, DIM), F32, kind="Internal").ap()
    y_rows = nc.dram_tensor("y_rows", (BLOCKS * P, DIM), F32, kind="Internal").ap()

    with ExitStack() as ctx:
        def sb(name, shape, dt=F32):
            return ctx.enter_context(nc.sbuf_tensor(name, shape, dt))

        def sem(name):
            return ctx.enter_context(nc.semaphore(name))

        bank = [ctx.enter_context(nc.psum_tensor(f"bank{i}", [P, 512], F32)) for i in range(8)]

        w12_sb = sb("w12_sb", [P, E * W12])
        w3_sb = sb("w3_sb", [P, E * DIM])
        sw3_sb = sb("sw3_sb", [P, IC, DIM])
        rw_sb = sb("rw_sb", [P, KC, E])
        b3s_sb = sb("b3s_sb", [E + 1, DIM])
        condb_sb = sb("condb_sb", [P, DIM])
        rb_sb = sb("rb_sb", [P, E])
        rbias_sb = sb("rbias_sb", [P, E])
        sb12_sb = sb("sb12_sb", [P, 2, IC])

        region1 = sb("region1", [P, KC * T])
        xT_sb = region1[:].rearrange("p (k t) -> p k t", k=KC)
        b12_sb = region1[:]
        region2 = sb("region2", [P, 6144])
        lora_sb = region2[:, 0:4096].rearrange("p (g c) -> p g c", g=GROUPS_L)
        loraA_sb = region2[:, 4096:6144].rearrange("p (g k r) -> p g k r", g=GROUPS_L, k=KC)
        onehot_off = region2[:, 0:2048].rearrange("p (j o) -> p j o", o=P)
        hsT_sb = region2[:, 2048:4096].rearrange("p (c t) -> p c t", c=IC)
        xg_sb = region2[:, 4096:6144].rearrange("p (s c) -> p s c", s=4)
        blk_tok = region2[:, 4096:4608].rearrange("p (k i b) -> p k i b", k=K, i=TILES)
        selpos = region2[:, 4608:4864].rearrange("p (k i e) -> p k i e", k=K, i=TILES)
        region3 = sb("region3", [P, 4096])
        condW_sb = region3[:, 0:2048].rearrange("p (k o) -> p k o", k=KC)
        xt_sb = region3[:, 2048:4096].rearrange("p (s o) -> p s o", s=4)
        x_sb = region3[:].rearrange("p (i o) -> p i o", i=TILES)
        region5 = sb("region5", [P, 2048])
        sw12_sb = region5[:].rearrange("p (m k c) -> p m k c", m=2, k=KC)
        xgT_sb = region5[:, 0:1024].rearrange("p (s k t) -> p s k t", s=2, k=KC)
        y_sb = region5[:, 1024:2048].rearrange("p (s o) -> p s o", s=2)
        region6 = sb("region6", [P, 1024])
        sg_sb = region6[:].rearrange("p (s o) -> p s o", s=2)
        pre_sb = region6[:, 0:512].rearrange("p (s o) -> p s o", s=2)
        gl_sb = region6[:, 512:768].rearrange("p (s o) -> p s o", s=2)
        h_sb = region6[:, 768:1024].rearrange("p (s o) -> p s o", s=2)
        region4 = sb("region4", [P, KC * T])
        xtT_sb = region4[:].rearrange("p (k t) -> p k t", k=KC)
        yg_sb = region4[:].rearrange("p (s k c) -> p s k c", s=4, k=K)

        lh_sb = sb("lh_sb", [P, 2, P])
        lhT_sb = sb("lhT_sb", [P, 2, P])
        hT_sb = lhT_sb

        ident = sb("ident", [P, P])
        upper = sb("upper", [P, P])
        ones = sb("ones", [P, P])
        lmask = sb("lmask", [P, SEQ_PER_TILE, RANK])
        tri16 = sb("tri16", [P, E, E])
        tri4 = sb("tri4", [P, GROUPS, GROUPS])
        cols_i = sb("cols_i", [P, P], I32)
        cols = sb("cols", [P, P])
        part_i = sb("part_i", [P, 1], I32)
        part16_i = sb("part16_i", [P, 1], I32)
        part16 = sb("part16", [P, 1])
        tok_i = sb("tok_i", [P, TILES], I32)
        tok = sb("tok", [P, TILES])
        thr = sb("thr", [P, TILES])
        desc = sb("desc", [P, E])

        slot_i = sb("slot_i", [P, GROUPS_L], I32)
        slot_f = sb("slot_f", [P, GROUPS_L])
        slot_f2 = sb("slot_f2", [P, GROUPS_L])
        lora_row = sb("lora_row", [P, GROUPS_L], I32)
        lg = sb("lg", [P, TILES, E])
        lgs = sb("lgs", [P, TILES, E])
        ex = sb("ex", [P, TILES, E])
        sc = sb("sc", [P, TILES, E])
        sc1 = sb("sc1", [P, TILES, E])
        tmp = sb("tmp", [P, TILES, E])
        red = sb("red", [P, TILES])
        red2 = sb("red2", [P, TILES])
        gmax = sb("gmax", [P, TILES, GROUPS])
        gcmp = sb("gcmp", [P, TILES, GROUPS, GROUPS])
        geq = sb("geq", [P, TILES, GROUPS, GROUPS])
        gpen = sb("gpen", [P, TILES, GROUPS])
        sel = sb("sel", [P, K, TILES, E])
        val = sb("val", [P, K, TILES])
        chosen = sb("chosen", [P, TILES, E])
        gate = sb("gate", [P, TILES, E + 1])
        gateT = sb("gateT", [E + 1, T])
        cnt = sb("cnt", [P, E])
        ncmp = sb("ncmp", [P, E, E])
        nblk = sb("nblk", [P, E])
        base = sb("base", [P, E])
        ends = sb("ends", [P, E])
        ecmp = condb_sb[0:1, :].rearrange("p (b e) -> p b e", e=E)
        eid_f = sb("eid_f", [1, BPAD])
        eid = sb("eid", [1, BPAD], I32)
        rank = sb("rank", [P, TILES, E])
        pos = sb("pos", [P, K * TILES])
        pos_i = sb("pos_i", [P, K * TILES], I32)
        off_i = sb("off_i", [P, K * TILES], I32)
        blk_i = sb("blk_i", [P, K * TILES], I32)
        off = sb("off", [P, K * TILES])
        blk = sb("blk", [P, K * TILES])
        slot_tok = sb("slot_tok", [P, BPAD], I32)

        condW_in, seq_in, small_in, x_in = sem("condW_in"), sem("seq_in"), sem("small_in"), sem("x_in")
        xT_in = [sem(f"xT_in{c}") for c in range(XCHUNKS)]
        shared_in, experts_in, b12_in = sem("shared_in"), sem("experts_in"), sem("b12_in")
        lora_in = [sem(f"lora_in{g}") for g in range(GROUPS_L)]
        pool_step, consts_ready, consts_f = sem("pool_step"), sem("consts_ready"), sem("consts_f")
        lora_row_ready = sem("lora_row_ready")
        loraA_turned, loraA_copied = sem("loraA_turned"), sem("loraA_copied")
        lh_done, lh_masked, lhT_done, lhT_copied = sem("lh_done"), sem("lh_masked"), sem("lhT_done"), sem("lhT_copied")
        cond_done, xt_ready, xtT_done, xtT_copied = sem("cond_done"), sem("xt_ready"), sem("xtT_done"), sem("xtT_copied")
        xt_stored = [sem(f"xt_stored{s}") for s in range(4)]
        logits_done, shifted, exp_done, dve_step = sem("logits_done"), sem("shifted"), sem("exp_done"), sem("dve_step")
        chosen_ready, ranks_done, onehots_ready, slots_done = (
            sem("chosen_ready"), sem("ranks_done"), sem("onehots_ready"), sem("slots_done"))
        slot_tok_ready, eid_ready, gate_ready, gateT_done, gateT_copied = (
            sem("slot_tok_ready"), sem("eid_ready"), sem("gate_ready"), sem("gateT_done"), sem("gateT_copied"))
        sh_gate_done, sh_up_done, sh_silu, sh_hidden = (
            sem("sh_gate_done"), sem("sh_up_done"), sem("sh_silu"), sem("sh_hidden"))
        gathered = [sem(f"gathered{s}") for s in range(4)]
        xg_turned, xgT_copied, a_done, pre_ready, act_ready, h_ready = (
            sem("xg_turned"), sem("xgT_copied"), sem("a_done"), sem("pre_ready"), sem("act_ready"), sem("h_ready"))
        h_turned, hT_copied, y_done, y_copied = sem("h_turned"), sem("hT_copied"), sem("y_done"), sem("y_copied")
        y_stored = [sem(f"y_stored{s}") for s in range(2)]
        shared_done, acc_shared, y_in = sem("shared_done"), sem("acc_shared"), [sem(f"y_in{s}") for s in range(4)]
        acc_done, out_stored = sem("acc_done"), sem("out_stored")

        def cond_bank(i):
            return bank[(0, 1, 7)[i % 3]]

        def shared_bank(i):
            return bank[(7, 0, 1, 2)[i % 4]]

        block = ctx.enter_context(nc.Block())

        @block.sync
        def _(sp):
            sp.dma_start(slot_i[:], seq_slot).then_inc(seq_in, 16)
            sp.dma_start(condW_sb, condWT.rearrange("k p o -> p k o")).then_inc(condW_in, 16)
            for c in range(XCHUNKS):
                sp.dma_start(xT_sb[:, :, c * CH:(c + 1) * CH],
                             xT.rearrange("k p t -> p k t")[:, :, c * CH:(c + 1) * CH]).then_inc(xT_in[c], 16)
                if c == 0:
                    sp.dma_start(condb_sb[:], cond_b.partition_broadcast(P)).then_inc(small_in, 16)
                    sp.dma_start(rw_sb[:], router_w).then_inc(small_in, 16)
                    sp.dma_start(rb_sb[:], router_b.partition_broadcast(P)).then_inc(small_in, 16)
                    sp.dma_start(rbias_sb[:], router_bias.partition_broadcast(P)).then_inc(small_in, 16)
                    sp.dma_start(sb12_sb[:], sb12).then_inc(small_in, 16)
                    sp.dma_start(b3s_sb[:], b3s).then_inc(small_in, 16)
            sp.dma_start(sw12_sb, sw12).then_inc(shared_in, 16)
            sp.dma_start(sw3_sb[:], sw3).then_inc(shared_in, 16)
            for i in range(TILES):
                sp.wait_ge(xt_ready, i + 1)
                sp.dma_start(xt_rows[i * P:(i + 1) * P, :], xt_sb[:, i % 4, :]).then_inc(xt_stored[i % 4], 16)
            sp.wait_ge(cond_done, TILES)
            sp.dma_start(b12_sb, b12.partition_broadcast(P)).then_inc(b12_in, 16)
            sp.wait_ge(xtT_done, TILES)
            for s in range(4):
                sp.wait_ge(xt_stored[s], 16 * TILES // 4)
            sp.dma_start(x_sb, x.rearrange("(i p) d -> p i d", p=P)).then_inc(x_in, 16)

            def store_y(b, s):
                sp.wait_ge(y_copied, b + 1)
                sp.dma_start(y_rows[bass.ds(b * P, P), :], y_sb[:, s % 2, :]).then_inc(y_stored[s % 2], 16)

            for b in range(UNROLL):
                store_y(b, b)
            with sp.Fori(UNROLL, BLOCKS - BLOCKS % UNROLL, UNROLL) as b:
                for s in range(UNROLL):
                    store_y(b + s, s)
            for b in range(BLOCKS - BLOCKS % UNROLL, BLOCKS):
                store_y(b, b)
            for i in range(TILES):
                sp.wait_ge(acc_done, i + 1)
                sp.dma_start(out[i * P:(i + 1) * P, :], x_sb[:, i, :]).then_inc(out_stored, 16)
            sp.wait_ge(out_stored, 16 * TILES)

        @block.gpsimd
        def _(pool):
            pool.iota(part_i[:], pattern=[[0, 1]], base=0, channel_multiplier=1).then_inc(consts_ready, 1)
            pool.iota(cols_i[:], pattern=[[1, P]], base=0, channel_multiplier=0).then_inc(consts_ready, 1)
            pool.iota(tok_i[:], pattern=[[P, TILES]], base=0, channel_multiplier=1).then_inc(consts_ready, 1)
            pool.memset(ident[:], 0.0).then_inc(pool_step, 1)
            pool.memset(lmask[:], LORA_SCALE).then_inc(pool_step, 1)
            pool.memset(ones[:], 1.0).then_inc(pool_step, 1)
            pool.memset(tri16[:], 1.0).then_inc(pool_step, 1)
            pool.memset(tri4[:], 1.0).then_inc(pool_step, 1)
            pool.memset(lh_sb[:], 0.0).then_inc(pool_step, 1)
            pool.wait_ge(pool_step, 6)
            pool.affine_select(out=ident[:], in_=ident[:], compare_op=ALU.not_equal, fill=1.0, base=0,
                               pattern=[[-1, P]], channel_multiplier=1).then_inc(consts_ready, 1)
            pool.affine_select(out=lmask[:], in_=lmask[:], compare_op=ALU.is_ge, fill=0.0, base=0,
                               pattern=[[-SEQ_LEN, SEQ_PER_TILE], [0, RANK]],
                               channel_multiplier=1).then_inc(pool_step, 1)
            pool.wait_ge(pool_step, 7)
            pool.affine_select(out=lmask[:], in_=lmask[:], compare_op=ALU.is_ge, fill=0.0, base=SEQ_LEN - 1,
                               pattern=[[SEQ_LEN, SEQ_PER_TILE], [0, RANK]],
                               channel_multiplier=-1).then_inc(consts_ready, 1)
            pool.wait_ge(lora_row_ready, 1)
            for g in range(GROUPS_L):
                pool.indirect_dma_start(lora_sb[:, g, :], None, lora,
                                        bass.IndirectOffsetOnAxis(ap=lora_row[:, g:g + 1], axis=0)).then_inc(lora_in[g], 16)
            pool.affine_select(out=upper[:], in_=ones[:], compare_op=ALU.is_gt, fill=0.0, base=0,
                               pattern=[[1, P]], channel_multiplier=-1).then_inc(consts_ready, 1)
            pool.affine_select(out=tri16[:], in_=tri16[:], compare_op=ALU.is_gt, fill=0.0, base=0,
                               pattern=[[1, E], [-1, E]], channel_multiplier=0).then_inc(consts_ready, 1)
            pool.affine_select(out=tri4[:], in_=tri4[:], compare_op=ALU.is_gt, fill=0.0, base=0,
                               pattern=[[1, GROUPS], [-1, GROUPS]], channel_multiplier=0).then_inc(consts_ready, 1)

            pool.wait_ge(slot_tok_ready, 1)
            for s in range(4):
                pool.wait_ge(xt_stored[s], 16 * TILES // 4)
            for b in range(BLOCKS):
                if b >= 4:
                    pool.wait_ge(xg_turned, b - 3)
                pool.indirect_dma_start(xg_sb[:, b % 4, :], None, xt_rows,
                                        bass.IndirectOffsetOnAxis(ap=slot_tok[:, b:b + 1], axis=0)
                                        ).then_inc(gathered[b % 4], 16)
            pool.wait_ge(y_stored[0], 16 * ((BLOCKS + 1) // 2))
            pool.wait_ge(y_stored[1], 16 * (BLOCKS // 2))
            for i in range(TILES):
                if i >= 4:
                    pool.wait_ge(acc_done, i - 3)
                for k in range(K):
                    j = k * TILES + i
                    pool.indirect_dma_start(yg_sb[:, i % 4, k, :], None, y_rows,
                                            bass.IndirectOffsetOnAxis(ap=pos_i[:, j:j + 1], axis=0)
                                            ).then_inc(y_in[i % 4], 16)

        @block.scalar
        def _(act):
            act.wait_ge(xT_in[1], 16)
            for e in range(E):
                act.dma_start(w12_sb[:, e * W12:(e + 1) * W12], w12[e]).then_inc(experts_in, 16)
                act.dma_start(w3_sb[:, e * DIM:(e + 1) * DIM], w3[e]).then_inc(experts_in, 16)
            for g in range(GROUPS_L):
                act.wait_ge(loraA_turned, g + 1)
                act.copy(loraA_sb[:, g], bank[2 + g][:].rearrange("p (k r) -> p k r", k=KC)).then_inc(loraA_copied, 1)

            def copy_lhT(i):
                act.wait_ge(lhT_done, i + 1)
                act.copy(lhT_sb[:, i % 2, :], bank[5][:, 0:P]).then_inc(lhT_copied, 1)

            def copy_xtT(i):
                act.wait_ge(xtT_done, i + 1)
                act.copy(xtT_sb[:, :, i * P:(i + 1) * P],
                         bank[2 + i % 2][:].rearrange("p (k t) -> p k t", k=KC)).then_inc(xtT_copied, 1)

            for i in range(TILES):
                copy_lhT(i)
                if i >= 1:
                    copy_xtT(i - 1)
            copy_xtT(TILES - 1)

            act.wait_ge(shifted, 1)
            act.activation(ex[:], lgs[:], ACT.Exp).then_inc(exp_done, 1)
            for u in range(2 * IC):
                act.wait_ge(sh_gate_done, u + 1)
                if u >= 2:
                    act.wait_ge(sh_hidden, u - 1)
                act.activation(sg_sb[:, u % 2, :], bank[2 * (u % 2)][:], ACT.Silu,
                               bias=sb12_sb[:, 0, u % IC:u % IC + 1]).then_inc(sh_silu, 1)
            for n in range(2):
                act.wait_ge(gateT_done, n + 1)
                act.copy(gateT[:, n * 512:(n + 1) * 512], bank[6 + n][0:E + 1, :]).then_inc(gateT_copied, 1)

            def copy_xgT(b, s):
                act.wait_ge(xg_turned, b + 1)
                act.copy(xgT_sb[:, s % 2], bank[s % 2][:].rearrange("p (k t) -> p k t", k=KC)).then_inc(xgT_copied, 1)

            def silu(b, s):
                act.wait_ge(pre_ready, b + 1)
                act.activation(gl_sb[:, s % 2, :], pre_sb[:, s % 2, 0:INTER], ACT.Silu).then_inc(act_ready, 1)

            def copy_hT(b, s):
                act.wait_ge(h_turned, b + 1)
                act.copy(hT_sb[:, s % 2, :], bank[4][:, 0:P]).then_inc(hT_copied, 1)

            def steps(b, s):
                copy_hT(b, s)
                copy_xgT(b + 2, s + 2)
                silu(b + 1, s + 1)

            copy_xgT(0, 0)
            copy_xgT(1, 1)
            silu(0, 0)
            with act.Fori(0, BLOCKS - BLOCKS % UNROLL, UNROLL) as b:
                for s in range(UNROLL):
                    steps(b + s, s)
            for b in range(BLOCKS - BLOCKS % UNROLL, BLOCKS):
                copy_hT(b, b)
                if b + 2 < BLOCKS:
                    copy_xgT(b + 2, b + 2)
                if b + 1 < BLOCKS:
                    silu(b + 1, b + 1)

        @block.vector
        def _(dve):
            made = [0]

            def then(ins):
                made[0] += 1
                ins.then_inc(dve_step, 1)
                dve.wait_ge(dve_step, made[0])

            def over_tiles(ap):
                return ap.unsqueeze(1).to_broadcast([P, TILES, E])

            def over_experts(ap):
                return ap.unsqueeze(2).to_broadcast([P, TILES, E])

            dve.wait_ge(consts_ready, 3)
            then(dve.tensor_scalar(part16_i[:], part_i[:], RANK - 1, None, ALU.bitwise_and))
            then(dve.tensor_copy(part16[:], part16_i[:]))
            dve.wait_ge(seq_in, 16)
            then(dve.tensor_copy(slot_f[:], slot_i[:]))
            then(dve.tensor_scalar(slot_f2[:], slot_f[:], float(RANK), None, ALU.mult))
            dve.tensor_scalar(lora_row[:], slot_f2[:], part16[:, 0:1], None, ALU.add).then_inc(lora_row_ready, 1)
            then(dve.tensor_copy(cols[:], cols_i[:]))
            then(dve.tensor_copy(tok[:], tok_i[:]))
            then(dve.tensor_scalar(thr[:], cols[:, 0:TILES], float(P), None, ALU.mult))
            then(dve.tensor_scalar(desc[:], cols[:, 0:E], -1.0, float(E), ALU.mult, ALU.add))
            dve.memset(gate[:, :, E:E + 1], 1.0).then_inc(consts_f, 1)

            dve.wait_ge(consts_ready, 5)
            dve.wait_ge(small_in, 16 * 6)
            for i in range(TILES):
                dve.wait_ge(lh_done, i + 1)
                c = LR * (i % 2)
                dve.tensor_tensor(lh_sb[:, i % 2, c:c + LR], bank[4][:, 0:LR],
                                  lmask[:].rearrange("p q r -> p (q r)"), ALU.mult).then_inc(lh_masked, 1)
                dve.wait_ge(cond_done, i + 1)
                if i >= 4:
                    dve.wait_ge(xt_stored[i % 4], 16 * (i // 4))
                dve.tensor_tensor(xt_sb[:, i % 4, :], cond_bank(i)[:], condb_sb[:], ALU.add).then_inc(xt_ready, 1)

            def hidden(u):
                dve.wait_ge(sh_up_done, u + 1)
                dve.wait_ge(sh_silu, u + 1)
                n, c = u // IC, u % IC
                dve.scalar_tensor_tensor(out=hsT_sb[:, c, n * HALF:(n + 1) * HALF], in0=bank[2 * (u % 2) + 1][:],
                                         scalar=sb12_sb[:, 1, c:c + 1], in1=sg_sb[:, u % 2, :],
                                         op0=ALU.add, op1=ALU.mult).then_inc(sh_hidden, 1)

            dve.wait_ge(consts_ready, 8)
            dve.wait_ge(logits_done, 1)
            then(dve.tensor_tensor(lg[:], bank[6][:, 0:TILES * E].rearrange("p (i e) -> p i e", e=E),
                                   over_tiles(rb_sb[:]), ALU.add))
            then(dve.tensor_reduce(red[:], lg[:], AX.X, ALU.max))
            dve.tensor_tensor(lgs[:], lg[:], over_experts(red[:]), ALU.subtract).then_inc(shifted, 1)
            dve.wait_ge(exp_done, 1)
            then(dve.tensor_reduce(red[:], ex[:], AX.X, ALU.add))
            then(dve.reciprocal(red2[:], red[:]))
            then(dve.tensor_tensor(tmp[:], ex[:], over_experts(red2[:]), ALU.mult))
            then(dve.tensor_tensor(sc[:], tmp[:], over_tiles(rbias_sb[:]), ALU.add))
            then(dve.tensor_reduce(gmax[:], sc[:].rearrange("p i (g m) -> p i g m", m=PER_GROUP), AX.X, ALU.max))
            pair = [P, TILES, GROUPS, GROUPS]
            mine, other = gmax[:].unsqueeze(3).to_broadcast(pair), gmax[:].unsqueeze(2).to_broadcast(pair)
            then(dve.tensor_tensor(gcmp[:], other, mine, ALU.is_gt))
            then(dve.tensor_tensor(geq[:], other, mine, ALU.is_equal))
            then(dve.tensor_tensor(geq[:], geq[:], tri4[:].unsqueeze(1).to_broadcast(pair), ALU.mult))
            then(dve.tensor_tensor(gcmp[:], gcmp[:], geq[:], ALU.add))
            then(dve.tensor_reduce(gpen[:], gcmp[:], AX.X, ALU.add))
            then(dve.tensor_scalar(gpen[:], gpen[:], float(LIM), -BIG, ALU.is_ge, ALU.mult))
            then(dve.tensor_tensor(sc1[:].rearrange("p i (g m) -> p i g m", m=PER_GROUP),
                                   sc[:].rearrange("p i (g m) -> p i g m", m=PER_GROUP),
                                   gpen[:].unsqueeze(3).to_broadcast([P, TILES, GROUPS, PER_GROUP]), ALU.add))
            for k in range(K):
                then(dve.tensor_reduce(val[:, k, :], sc1[:], AX.X, ALU.max))
                then(dve.tensor_tensor(tmp[:], sc1[:], over_experts(val[:, k, :]), ALU.is_equal))
                then(dve.tensor_tensor(tmp[:], tmp[:], over_tiles(desc[:]), ALU.mult))
                then(dve.tensor_reduce(red[:], tmp[:], AX.X, ALU.max))
                then(dve.tensor_tensor(sel[:, k], over_tiles(desc[:]), over_experts(red[:]), ALU.is_equal))
                if k == 0:
                    then(dve.scalar_tensor_tensor(out=sc1[:], in0=sel[:, 0], scalar=-BIG, in1=sc1[:],
                                                  op0=ALU.mult, op1=ALU.add))
            dve.tensor_tensor(chosen[:], sel[:, 0], sel[:, 1], ALU.add).then_inc(chosen_ready, 1)
            then(dve.tensor_tensor(tmp[:], sel[:, 0], over_experts(val[:, 0, :]), ALU.mult))
            then(dve.tensor_tensor(sc1[:], sel[:, 1], over_experts(val[:, 1, :]), ALU.mult))
            dve.tensor_tensor(gate[:, :, 0:E], tmp[:], sc1[:], ALU.add).then_inc(gate_ready, 1)
            hidden(0)

            dve.wait_ge(cond_done, TILES)
            dve.wait_ge(ranks_done, 1)
            then(dve.tensor_reduce(cnt[:], bank[4][:, P:2 * P].rearrange("p (i e) -> p e i", e=E), AX.X, ALU.add))
            cmp8 = [P, E, TILES]
            then(dve.tensor_tensor(ncmp[:, :, 0:TILES], cnt[:].unsqueeze(2).to_broadcast(cmp8),
                                   thr[:].unsqueeze(1).to_broadcast(cmp8), ALU.is_gt))
            then(dve.tensor_reduce(nblk[:], ncmp[:, :, 0:TILES], AX.X, ALU.add))
            then(dve.tensor_tensor(ncmp[:], nblk[:].unsqueeze(1).to_broadcast([P, E, E]), tri16[:], ALU.mult))
            then(dve.tensor_reduce(base[:], ncmp[:], AX.X, ALU.add))
            then(dve.scalar_tensor_tensor(out=rank[:], in0=over_tiles(base[:]), scalar=float(P),
                                          in1=bank[4][:, 0:P].rearrange("p (i e) -> p i e", e=E),
                                          op0=ALU.mult, op1=ALU.add))
            then(dve.tensor_tensor(selpos, sel[:], rank[:].unsqueeze(1).to_broadcast([P, K, TILES, E]), ALU.mult))
            then(dve.tensor_reduce(pos[:], selpos.rearrange("p k i e -> p (k i) e"), AX.X, ALU.add))
            then(dve.tensor_copy(pos_i[:], pos[:]))
            then(dve.tensor_scalar(off_i[:], pos_i[:], P - 1, None, ALU.bitwise_and))
            then(dve.tensor_scalar(blk_i[:], pos_i[:], P.bit_length() - 1, None, ALU.arith_shift_right))
            then(dve.tensor_copy(off[:], off_i[:]))
            then(dve.tensor_copy(blk[:], blk_i[:]))
            NJ = K * TILES
            dve.tensor_tensor(onehot_off, off[:].unsqueeze(2).to_broadcast([P, NJ, P]),
                              cols[:].unsqueeze(1).to_broadcast([P, NJ, P]), ALU.is_equal).then_inc(onehots_ready, 1)
            flat = blk_tok.rearrange("p k i b -> p (k i) b")
            then(dve.tensor_tensor(flat, blk[:].unsqueeze(2).to_broadcast([P, NJ, BPAD]),
                                   cols[:, 0:BPAD].unsqueeze(1).to_broadcast([P, NJ, BPAD]), ALU.is_equal))
            tok_b = tok[:].unsqueeze(1).unsqueeze(3).to_broadcast([P, K, TILES, BPAD])
            dve.tensor_tensor(blk_tok, blk_tok, tok_b, ALU.mult).then_inc(onehots_ready, 1)
            then(dve.tensor_tensor(ends[:], base[:], nblk[:], ALU.add))
            then(dve.tensor_tensor(ecmp, ends[0:1, :].unsqueeze(1).to_broadcast([1, BPAD, E]),
                                   cols[0:1, 0:BPAD].unsqueeze(2).to_broadcast([1, BPAD, E]), ALU.is_le))
            then(dve.tensor_reduce(eid_f[:], ecmp, AX.X, ALU.add))
            then(dve.tensor_scalar(eid[:], eid_f[:], float(E - 1), None, ALU.min))
            dve.engine_nop().then_inc(eid_ready, 1)
            hidden(1)
            dve.wait_ge(slots_done, 1)
            dve.tensor_copy(slot_tok[:], bank[5][:, 0:BPAD]).then_inc(slot_tok_ready, 1)
            hidden(2)
            hidden(3)

            dve.wait_ge(b12_in, 16)

            def add_bias(b, s):
                e = dve.value_load(eid[0:1, bass.ds(b, 1)], min_val=0, max_val=E - 1)
                dve.wait_ge(a_done, b + 1)
                dve.tensor_tensor(pre_sb[:, s % 2, :], bank[2 + s % 2][:, 0:2 * INTER],
                                  b12_sb[:, bass.ds(e * (2 * INTER), 2 * INTER)], ALU.add).then_inc(pre_ready, 1)

            def times_up(b, s):
                dve.wait_ge(act_ready, b + 1)
                dve.tensor_tensor(h_sb[:, s % 2, :], gl_sb[:, s % 2, :], pre_sb[:, s % 2, INTER:], ALU.mult).then_inc(h_ready, 1)

            def copy_y(b, s):
                dve.wait_ge(y_done, b + 1)
                if not (isinstance(b, int) and b < 2):
                    dve.wait_ge(y_stored[s % 2], (b - s % 2) * 8)
                dve.tensor_copy(y_sb[:, s % 2, :], bank[5 + s % 2][:]).then_inc(y_copied, 1)

            add_bias(0, 0)
            times_up(0, 0)
            for b in range(UNROLL):
                add_bias(b + 1, b + 1)
                times_up(b + 1, b + 1)
                copy_y(b, b)
            with dve.Fori(UNROLL, BLOCKS - BLOCKS % UNROLL, UNROLL) as b:
                for s in range(UNROLL):
                    add_bias(b + (s + 1), s + 1)
                    times_up(b + (s + 1), s + 1)
                    copy_y(b + s, s)
            for b in range(BLOCKS - BLOCKS % UNROLL, BLOCKS):
                if b + 1 < BLOCKS:
                    add_bias(b + 1, b + 1)
                    times_up(b + 1, b + 1)
                copy_y(b, b)

            dve.wait_ge(x_in, 16)

            def add_shared(i):
                dve.wait_ge(shared_done, i + 1)
                dve.tensor_tensor(x_sb[:, i, :], x_sb[:, i, :], shared_bank(i)[:], ALU.add).then_inc(acc_shared, 1)

            def add_experts(i):
                dve.wait_ge(y_in[i % 4], 16 * K * (i // 4 + 1))
                dve.wait_ge(acc_shared, i + 1)
                for k in range(K):
                    ins = dve.scalar_tensor_tensor(out=x_sb[:, i, :], in0=yg_sb[:, i % 4, k, :],
                                                   scalar=val[:, k, i:i + 1], in1=x_sb[:, i, :],
                                                   op0=ALU.mult, op1=ALU.add)
                    if k < K - 1:
                        then(ins)
                ins.then_inc(acc_done, 1)

            for i in range(TILES):
                add_shared(i)
                if i >= 2:
                    add_experts(i - 2)
            add_experts(TILES - 2)
            add_experts(TILES - 1)

        @block.tensor
        def _(pe):
            def cond_w(i):
                if i % 2 == 0:
                    pe.wait_ge(xT_in[i // 2], 16)
                if i >= 3:
                    pe.wait_ge(xt_ready, i - 2)
                for k in range(KC):
                    pe.matmul(cond_bank(i)[:], xT_sb[:, k, i * P:(i + 1) * P], condW_sb[:, k, :],
                              start=(k == 0), stop=False)

            def lora_h(i):
                g, j = i // 2, i % 2
                if i == 0:
                    pe.wait_ge(loraA_copied, 4)
                for k in range(KC):
                    mm = pe.matmul(bank[4][:, 0:LR], xT_sb[:, k, i * P:(i + 1) * P],
                                   loraA_sb[:, g, k, LR * j:LR * (j + 1)], start=(k == 0), stop=(k == KC - 1))
                mm.then_inc(lh_done, 1)

            def turn_lora_h(i):
                pe.wait_ge(lh_masked, i + 1)
                pe.transpose(bank[5][:, 0:P], lh_sb[:, i % 2, :], ident[:]).then_inc(lhT_done, 1)

            def cond_lora(i):
                pe.wait_ge(lhT_copied, i + 1)
                pe.matmul(cond_bank(i)[:], lhT_sb[:, i % 2, :], lora_sb[:, i // 2, DIM:2 * DIM],
                          start=False, stop=True).then_inc(cond_done, 1)

            def turn_xt(i):
                pe.wait_ge(xt_ready, i + 1)
                if i >= 2:
                    pe.wait_ge(xtT_copied, i - 1)
                for k in range(KC):
                    mm = pe.transpose(bank[2 + i % 2][:, k * P:(k + 1) * P], xt_sb[:, i % 4, k * P:(k + 1) * P], ident[:])
                mm.then_inc(xtT_done, 1)

            def logits(i):
                pe.wait_ge(xtT_copied, i + 1)
                for k in range(KC):
                    mm = pe.matmul(bank[6][:, i * E:(i + 1) * E], xtT_sb[:, k, i * P:(i + 1) * P], rw_sb[:, k, :],
                                   start=(k == 0), stop=(k == KC - 1))
                if i == TILES - 1:
                    mm.then_inc(logits_done, 1)

            pe.wait_ge(condW_in, 16)
            cond_w(0)
            cond_w(1)
            pe.wait_ge(consts_ready, 4)
            for g in range(GROUPS_L):
                pe.wait_ge(lora_in[g], 16)
                for k in range(KC):
                    mm = pe.transpose(bank[2 + g][:, k * P:(k + 1) * P], lora_sb[:, g, k * P:(k + 1) * P], ident[:])
                mm.then_inc(loraA_turned, 1)
            pe.wait_ge(small_in, 16 * 6)
            for i in range(TILES):
                lora_h(i)
                if 1 <= i < TILES - 1:
                    cond_w(i + 1)
                turn_lora_h(i)
                if i >= 2:
                    logits(i - 2)
                if i >= 1:
                    turn_xt(i - 1)
                cond_lora(i)
            turn_xt(TILES - 1)
            logits(TILES - 2)
            logits(TILES - 1)

            def shared_up(u):
                n, c = u // IC, u % IC
                if u >= 2:
                    pe.wait_ge(sh_hidden, u - 1)
                for m, done in ((0, sh_gate_done), (1, sh_up_done)):
                    for k in range(KC):
                        mm = pe.matmul(bank[2 * (u % 2) + m][:], sw12_sb[:, m, k, c * P:(c + 1) * P],
                                       xtT_sb[:, k, n * HALF:(n + 1) * HALF], start=(k == 0), stop=(k == KC - 1))
                    mm.then_inc(done, 1)

            pe.wait_ge(shared_in, 32)
            shared_up(0)
            pe.wait_ge(chosen_ready, 1)
            pe.wait_ge(consts_ready, 8)
            flat = chosen[:].rearrange("p i e -> p (i e)")
            pe.matmul(bank[4][:, 0:P], upper[:], flat, start=True, stop=False)
            for i in range(TILES - 1):
                n = TILES - 1 - i
                pe.matmul(bank[4][:, (i + 1) * E:P], ones[:], chosen[:, i, :].unsqueeze(1).to_broadcast([P, n, E]),
                          start=False, stop=(i == TILES - 2))
            pe.matmul(bank[4][:, P:2 * P], ones[:], flat, start=True, stop=True).then_inc(ranks_done, 1)
            shared_up(1)
            shared_up(2)
            pe.wait_ge(onehots_ready, 2)
            for j in range(K * TILES):
                mm = pe.matmul(bank[5][:, 0:BPAD], onehot_off[:, j, :], blk_tok[:, j // TILES, j % TILES, :],
                               start=(j == 0), stop=(j == K * TILES - 1))
            mm.then_inc(slots_done, 1)
            pe.wait_ge(consts_f, 1)
            pe.wait_ge(gate_ready, 1)
            for i in range(TILES):
                mm = pe.transpose(bank[6 + i // 4][0:E + 1, (i % 4) * P:(i % 4 + 1) * P], gate[:, i, :], ident[:])
                if i % 4 == 3:
                    mm.then_inc(gateT_done, 1)
            shared_up(3)

            def turn_xg(b, s):
                pe.wait_ge(gathered[s % 4], ((b - s % 4) + 4) * 4)
                for k in range(KC):
                    mm = pe.transpose(bank[s % 2][:, k * P:(k + 1) * P], xg_sb[:, s % 4, k * P:(k + 1) * P], ident[:])
                mm.then_inc(xg_turned, 1)

            def expert_of(b):
                return pe.value_load(eid[0:1, bass.ds(b, 1)], min_val=0, max_val=E - 1)

            def up(b, s, e, first, last):
                if first == 0:
                    pe.wait_ge(xgT_copied, b + 1)
                for k in range(first, last):
                    mm = pe.matmul(bank[2 + s % 2][:, 0:2 * INTER], xgT_sb[:, s % 2, k, :],
                                   w12_sb[:, bass.ds(e * W12 + k * 2 * INTER, 2 * INTER)],
                                   start=(k == 0), stop=(k == KC - 1))
                if last == KC:
                    mm.then_inc(a_done, 1)

            def turn_h(b, s):
                pe.wait_ge(h_ready, b + 1)
                pe.transpose(bank[4][:, 0:P], h_sb[:, s % 2, :], ident[:]).then_inc(h_turned, 1)

            def down(b, s):
                e = expert_of(b)
                pe.wait_ge(hT_copied, b + 1)
                if not (isinstance(b, int) and b < 2):
                    pe.wait_ge(y_copied, b - 1)
                pe.matmul(bank[5 + s % 2][:], hT_sb[:, s % 2, :], w3_sb[:, bass.ds(e * DIM, DIM)],
                          start=True, stop=True).then_inc(y_done, 1)

            def steps(b, s):
                e = expert_of(b + 1)
                up(b + 1, s + 1, e, 0, KC // 2)
                turn_h(b, s)
                turn_xg(b + 2, s + 2)
                up(b + 1, s + 1, e, KC // 2, KC)
                down(b, s)

            pe.wait_ge(sh_hidden, 4)
            pe.wait_ge(slot_tok_ready, 1)
            pe.wait_ge(gateT_copied, 2)
            pe.wait_ge(eid_ready, 1)
            turn_xg(0, 0)
            turn_xg(1, 1)
            pe.wait_ge(experts_in, 16 * 2 * E)
            up(0, 0, expert_of(0), 0, KC)
            for b in range(UNROLL):
                steps(b, b)
            with pe.Fori(UNROLL, BLOCKS - BLOCKS % UNROLL, UNROLL) as b:
                for s in range(UNROLL):
                    steps(b + s, s)
            for b in range(BLOCKS - BLOCKS % UNROLL, BLOCKS):
                if b + 1 < BLOCKS:
                    e = expert_of(b + 1)
                    up(b + 1, b + 1, e, 0, KC // 2)
                turn_h(b, b)
                if b + 2 < BLOCKS:
                    turn_xg(b + 2, b + 2)
                if b + 1 < BLOCKS:
                    up(b + 1, b + 1, e, KC // 2, KC)
                down(b, b)

            for i in range(TILES):
                if i >= 4:
                    pe.wait_ge(acc_shared, i - 3)
                for c in range(IC):
                    pe.matmul(shared_bank(i)[:], hsT_sb[:, c, i * P:(i + 1) * P], sw3_sb[:, c, :],
                              start=(c == 0), stop=False)
                pe.matmul(shared_bank(i)[:], gateT[:, i * P:(i + 1) * P], b3s_sb[:], start=False, stop=True
                          ).then_inc(shared_done, 1)


def kernel(x, itok_B_0_23, L0_cond_W, L0_cond_b, L0_cond_lora_As, L0_cond_lora_Bs, L0_ffn_router_w,
           L0_ffn_router_b, L0_ffn_router_bias, L0_ffn_ew1, L0_ffn_eb1, L0_ffn_ew2, L0_ffn_eb2, L0_ffn_ew3,
           L0_ffn_eb3, L0_ffn_sw1, L0_ffn_sb1, L0_ffn_sw2, L0_ffn_sb2, L0_ffn_sw3, L0_ffn_sb3):
    import numpy as np
    import concourse.bacc as bacc
    from concourse.bass_utils import run_bass_kernel_spmd

    def chunks(w):
        w = np.asarray(w)
        return w.reshape(-1, P, w.shape[-1]).transpose(1, 0, 2)

    xf = np.asarray(x).reshape(T, DIM)
    w12 = np.concatenate([np.asarray(L0_ffn_ew1), np.asarray(L0_ffn_ew2)], axis=-1)
    w12 = w12.reshape(E, KC, P, 2 * INTER).transpose(0, 2, 1, 3).reshape(E, P, W12)
    laid = {
        "x": xf,
        "xT": xf.T.reshape(KC, P, T),
        "seq_slot": np.repeat(np.asarray(itok_B_0_23), RANK).reshape(GROUPS_L, P).T,
        "condWT": np.asarray(L0_cond_W).T.reshape(KC, P, DIM),
        "cond_b": np.asarray(L0_cond_b),
        "lora": np.concatenate([np.asarray(L0_cond_lora_As).transpose(0, 2, 1),
                                np.asarray(L0_cond_lora_Bs)], axis=-1).reshape(SLOTS * RANK, 2 * DIM),
        "router_w": chunks(L0_ffn_router_w),
        "router_b": np.asarray(L0_ffn_router_b),
        "router_bias": np.asarray(L0_ffn_router_bias),
        "w12": w12,
        "b12": np.concatenate([np.asarray(L0_ffn_eb1), np.asarray(L0_ffn_eb2)], axis=-1).reshape(-1),
        "w3": np.asarray(L0_ffn_ew3),
        "b3s": np.concatenate([np.asarray(L0_ffn_eb3), np.asarray(L0_ffn_sb3)[None]], axis=0),
        "sw12": np.stack([chunks(L0_ffn_sw1), chunks(L0_ffn_sw2)], axis=1),
        "sb12": np.stack([np.asarray(L0_ffn_sb1).reshape(IC, P).T, np.asarray(L0_ffn_sb2).reshape(IC, P).T], axis=1),
        "sw3": chunks(L0_ffn_sw3),
    }
    nc = bacc.Bacc("TRN2", target_bir_lowering=False, num_devices=1)
    arrays, args = {}, []
    for name, a in laid.items():
        a = np.ascontiguousarray(a)
        arrays[f"in_{name}"] = a
        args.append(nc.dram_tensor(f"in_{name}", a.shape, mybir.dt.from_np(a.dtype), kind="ExternalInput").ap())
    args.append(nc.dram_tensor("out_0", (T, DIM), F32, kind="ExternalOutput").ap())
    program(nc, *args)
    r = run_bass_kernel_spmd(nc, [arrays], core_ids=[0])
    return r.results[0]["out_0"].reshape(SEQS, SEQ_LEN, DIM)
```

```python
from contextlib import ExitStack

import concourse.bass as bass
from concourse import mybir

F32 = mybir.dt.float32
I32 = mybir.dt.int32
ALU = mybir.AluOpType
ACT = mybir.ActivationFunctionType
AX = mybir.AxisListType

P = 128
SEQS, SEQ_LEN, DIM = 32, 32, 512
T = SEQS * SEQ_LEN
TILES = T // P
KC = DIM // P
SLOTS, RANK = 32, 16
LORA_SCALE = 32 / RANK
SEQ_PER_TILE = P // SEQ_LEN
LR = SEQ_PER_TILE * RANK
GROUPS_L = SEQS * RANK // P
E, INTER, SHARED = 16, 128, 256
GROUPS, PER_GROUP, LIM, K = 4, 4, 2, 2
BLOCKS = (K * T + E * (P - 1)) // P
FULL = K * T // P
BPAD = 32
W12 = KC * 2 * INTER
IC = SHARED // P
HALF = T // 2
XCHUNKS = 4
CH = T // XCHUNKS
BIG = 3.0e38
UNROLL = 4
EXPERTS_PER_LOAD = 4
LOOP_END = BLOCKS - BLOCKS % UNROLL
DRAINED = BLOCKS - LOOP_END
assert LOOP_END == 28 and DRAINED == 3 and UNROLL == 4


def program(nc, x, xT, seq_slot, condWT, cond_b, lora, router_w, router_b, router_bias,
            w12, b12, w3, b3s, sw12, sb12, sw3, out):
    xt_rows = nc.dram_tensor("xt_rows", (T, DIM), F32, kind="Internal").ap()
    y_rows = nc.dram_tensor("y_rows", (K * T + BLOCKS * P, DIM), F32, kind="Internal").ap()

    with ExitStack() as ctx:
        def sb(name, shape, dt=F32):
            return ctx.enter_context(nc.sbuf_tensor(name, shape, dt))

        def sem(name):
            return ctx.enter_context(nc.semaphore(name))

        bank = [ctx.enter_context(nc.psum_tensor(f"bank{i}", [P, 512], F32)) for i in range(8)]

        w12_sb = sb("w12_sb", [P, E * W12])
        yg_sb = w12_sb[:, 0:TILES * K * DIM].rearrange("p (i k c) -> p i k c", i=TILES, k=K)
        w3_sb = sb("w3_sb", [P, E * DIM])
        sw3_sb = sb("sw3_sb", [P, IC, DIM])
        rw_sb = sb("rw_sb", [P, KC, E])
        b3s_sb = sb("b3s_sb", [E + 1, DIM])
        condb_sb = sb("condb_sb", [P, DIM])
        rb_sb = sb("rb_sb", [P, E])
        rbias_sb = sb("rbias_sb", [P, E])
        sb12_sb = sb("sb12_sb", [P, 2, IC])

        region1 = sb("region1", [P, KC * T])
        xT_sb = region1[:].rearrange("p (k t) -> p k t", k=KC)
        b12_sb = region1[:]
        region2 = sb("region2", [P, 6144])
        lora_sb = region2[:, 0:4096].rearrange("p (g c) -> p g c", g=GROUPS_L)
        loraA_sb = region2[:, 4096:6144].rearrange("p (g k r) -> p g k r", g=GROUPS_L, k=KC)
        onehot_off = region2[:, 0:2048].rearrange("p (j o) -> p j o", o=P)
        hsT_sb = region2[:, 2048:4096].rearrange("p (c t) -> p c t", c=IC)
        xg_sb = region2[:, 4096:6144].rearrange("p (s c) -> p s c", s=4)
        blk_tok = region2[:, 4096:4608].rearrange("p (k i b) -> p k i b", k=K, i=TILES)
        selpos = region2[:, 4608:4864].rearrange("p (k i e) -> p k i e", k=K, i=TILES)
        region3 = sb("region3", [P, 4096])
        condW_sb = region3[:, 0:2048].rearrange("p (k o) -> p k o", k=KC)
        xt_sb = region3[:, 2048:4096].rearrange("p (s o) -> p s o", s=4)
        x_sb = region3[:].rearrange("p (i o) -> p i o", i=TILES)
        region5 = sb("region5", [P, 2048])
        sw12_sb = region5[:].rearrange("p (m k c) -> p m k c", m=2, k=KC)
        xgT_sb = region5[:, 0:1024].rearrange("p (s k t) -> p s k t", s=2, k=KC)
        y_sb = region5[:, 1024:2048].rearrange("p (s o) -> p s o", s=2)
        region6 = sb("region6", [P, 1024])
        sg_sb = region6[:].rearrange("p (s o) -> p s o", s=2)
        pre_sb = region6[:, 0:512].rearrange("p (s o) -> p s o", s=2)
        gl_sb = region6[:, 512:768].rearrange("p (s o) -> p s o", s=2)
        h_sb = region6[:, 768:1024].rearrange("p (s o) -> p s o", s=2)
        region4 = sb("region4", [P, KC * T])
        xtT_sb = region4[:].rearrange("p (k t) -> p k t", k=KC)

        lh_sb = sb("lh_sb", [P, 2, P])
        lhT_sb = sb("lhT_sb", [P, 2, P])
        hT_sb = lhT_sb

        ident = sb("ident", [P, P])
        upper = sb("upper", [P, P])
        ones = sb("ones", [P, P])
        lmask = sb("lmask", [P, SEQ_PER_TILE, RANK])
        tri16 = sb("tri16", [P, E, E])
        tri4 = sb("tri4", [P, GROUPS, GROUPS])
        cols_i = sb("cols_i", [P, P], I32)
        cols = sb("cols", [P, P])
        part_i = sb("part_i", [P, 1], I32)
        part16_i = sb("part16_i", [P, 1], I32)
        part16 = sb("part16", [P, 1])
        slot_no_i = sb("slot_no_i", [P, BPAD], I32)
        thr = sb("thr", [P, TILES])
        desc = sb("desc", [P, E])

        slot_i = sb("slot_i", [P, GROUPS_L], I32)
        slot_f = sb("slot_f", [P, GROUPS_L])
        slot_f2 = sb("slot_f2", [P, GROUPS_L])
        lora_row = sb("lora_row", [P, GROUPS_L], I32)
        lg = sb("lg", [P, TILES, E])
        lgs = sb("lgs", [P, TILES, E])
        ex = sb("ex", [P, TILES, E])
        sc = sb("sc", [P, TILES, E])
        sc1 = sb("sc1", [P, TILES, E])
        tmp = sb("tmp", [P, TILES, E])
        red = sb("red", [P, TILES])
        red2 = sb("red2", [P, TILES])
        gmax = sb("gmax", [P, TILES, GROUPS])
        gcmp = sb("gcmp", [P, TILES, GROUPS, GROUPS])
        geq = sb("geq", [P, TILES, GROUPS, GROUPS])
        gpen = sb("gpen", [P, TILES, GROUPS])
        sel = sb("sel", [P, K, TILES, E])
        val = sb("val", [P, K, TILES])
        chosen = sb("chosen", [P, TILES, E])
        gate = sb("gate", [P, TILES, E + 1])
        gateT = sb("gateT", [E + 1, T])
        cnt = sb("cnt", [P, E])
        ncmp = sb("ncmp", [P, E, E])
        nblk = sb("nblk", [P, E])
        base = sb("base", [P, E])
        ends = sb("ends", [P, E])
        ecmp = condb_sb[0:1, :].rearrange("p (b e) -> p b e", e=E)
        eid_f = sb("eid_f", [1, BPAD])
        top_f = sb("top_f", [1, 1])
        nused = sb("nused", [1, 1], I32)
        eid = sb("eid", [1, BPAD + 1], I32)
        rows_stored = sem("rows_stored")
        rank = lgs
        pos = sb("pos", [P, K * TILES])
        pos_i = sb("pos_i", [P, K * TILES], I32)
        off_i = sb("off_i", [P, K * TILES], I32)
        blk_i = sb("blk_i", [P, K * TILES], I32)
        off = sb("off", [P, K * TILES])
        blk = sb("blk", [P, K * TILES])
        spent = ex[:].rearrange("p i e -> p (i e)")
        slot_f32, slot_empty, pair_row = spent[:, 0:BPAD], spent[:, BPAD:2 * BPAD], spent[:, 2 * BPAD:2 * BPAD + K * TILES]
        slot_tok = sb("slot_tok", [P, BPAD], I32)
        slot_row = sb("slot_row", [P, BPAD], I32)
        slot_no = sb("slot_no", [P, BPAD])

        condW_in, seq_in, small_in, x_in = sem("condW_in"), sem("seq_in"), sem("small_in"), sem("x_in")
        xT_in = [sem(f"xT_in{c}") for c in range(XCHUNKS)]
        shared_in, experts_in, b12_in = sem("shared_in"), sem("experts_in"), sem("b12_in")
        lora_in = [sem(f"lora_in{g}") for g in range(GROUPS_L)]
        pool_step, consts_ready, consts_f = sem("pool_step"), sem("consts_ready"), sem("consts_f")
        lora_row_ready = sem("lora_row_ready")
        loraA_turned, loraA_copied = sem("loraA_turned"), sem("loraA_copied")
        lh_done, lh_masked, lhT_done, lhT_copied = sem("lh_done"), sem("lh_masked"), sem("lhT_done"), sem("lhT_copied")
        cond_done, xt_ready, xtT_done, xtT_copied = sem("cond_done"), sem("xt_ready"), sem("xtT_done"), sem("xtT_copied")
        xt_stored = [sem(f"xt_stored{s}") for s in range(4)]
        logits_done, shifted, exp_done, dve_step = sem("logits_done"), sem("shifted"), sem("exp_done"), sem("dve_step")
        chosen_ready, ranks_done, onehots_ready, slots_done = (
            sem("chosen_ready"), sem("ranks_done"), sem("onehots_ready"), sem("slots_done"))
        slot_tok_ready, eid_ready, gate_ready, gateT_done, gateT_copied = (
            sem("slot_tok_ready"), sem("eid_ready"), sem("gate_ready"), sem("gateT_done"), sem("gateT_copied"))
        sh_gate_done, sh_up_done, sh_silu, sh_hidden = (
            sem("sh_gate_done"), sem("sh_up_done"), sem("sh_silu"), sem("sh_hidden"))
        gathered = [sem(f"gathered{s}") for s in range(4)]
        xg_turned, xgT_copied, a_done, pre_ready, act_ready, h_ready = (
            sem("xg_turned"), sem("xgT_copied"), sem("a_done"), sem("pre_ready"), sem("act_ready"), sem("h_ready"))
        h_turned, hT_copied, y_done, y_copied = sem("h_turned"), sem("hT_copied"), sem("y_done"), sem("y_copied")
        y_scattered = [sem(f"y_scattered{s}") for s in range(2)]
        shared_done, acc_shared, y_in = sem("shared_done"), sem("acc_shared"), [sem(f"y_in{i}") for i in range(TILES)]
        acc_done, out_stored = sem("acc_done"), sem("out_stored")

        def cond_bank(i):
            return bank[(0, 1, 7)[i % 3]]

        def shared_bank(i):
            return bank[(7, 0, 1, 2)[i % 4]]

        def last_group(eng):
            return eng.value_load(eid[0:1, BPAD:BPAD + 1], min_val=FULL - UNROLL, max_val=LOOP_END - UNROLL)

        block = ctx.enter_context(nc.Block())

        @block.sync
        def _(sp):
            sp.dma_start(slot_i[:], seq_slot).then_inc(seq_in, 16)
            sp.dma_start(condW_sb, condWT.rearrange("k p o -> p k o")).then_inc(condW_in, 16)
            for c in range(XCHUNKS):
                sp.dma_start(xT_sb[:, :, c * CH:(c + 1) * CH],
                             xT.rearrange("k p t -> p k t")[:, :, c * CH:(c + 1) * CH]).then_inc(xT_in[c], 16)
                if c == 0:
                    sp.dma_start(condb_sb[:], cond_b.partition_broadcast(P)).then_inc(small_in, 16)
                    sp.dma_start(rw_sb[:], router_w).then_inc(small_in, 16)
                    sp.dma_start(rb_sb[:], router_b.partition_broadcast(P)).then_inc(small_in, 16)
                    sp.dma_start(rbias_sb[:], router_bias.partition_broadcast(P)).then_inc(small_in, 16)
                    sp.dma_start(sb12_sb[:], sb12).then_inc(small_in, 16)
                    sp.dma_start(b3s_sb[:], b3s).then_inc(small_in, 16)
            sp.dma_start(sw12_sb, sw12).then_inc(shared_in, 16)
            sp.dma_start(sw3_sb[:], sw3).then_inc(shared_in, 16)
            for i in range(TILES):
                sp.wait_ge(xt_ready, i + 1)
                sp.dma_start(xt_rows[i * P:(i + 1) * P, :], xt_sb[:, i % 4, :]).then_inc(xt_stored[i % 4], 16)
            sp.wait_ge(cond_done, TILES)
            sp.dma_start(b12_sb, b12.partition_broadcast(P)).then_inc(b12_in, 16)
            sp.wait_ge(xtT_done, TILES)
            for s in range(4):
                sp.wait_ge(xt_stored[s], 16 * TILES // 4)
            sp.dma_start(x_sb, x.rearrange("(i p) d -> p i d", p=P)).then_inc(x_in, 16)
            sp.wait_ge(eid_ready, 1)
            top = last_group(sp)
            sp.wait_ge(y_scattered[0], (top + (UNROLL + DRAINED + 1)) * 8)
            sp.sem_inc(rows_stored, 1)
            sp.wait_ge(y_scattered[1], (top + (UNROLL + DRAINED - 1)) * 8)
            sp.sem_inc(rows_stored, 1)
            sp.wait_ge(rows_stored, 2)
            for i in range(TILES):
                sp.dma_start(yg_sb[:, i], y_rows[0:K * T, :].rearrange("(k i p) d -> i p k d", k=K, p=P)[i]
                             ).then_inc(y_in[i], 16)
            for i in range(TILES):
                sp.wait_ge(acc_done, i + 1)
                sp.dma_start(out[i * P:(i + 1) * P, :], x_sb[:, i, :]).then_inc(out_stored, 16)
            sp.wait_ge(out_stored, 16 * TILES)

        @block.gpsimd
        def _(pool):
            pool.iota(part_i[:], pattern=[[0, 1]], base=0, channel_multiplier=1).then_inc(consts_ready, 1)
            pool.iota(cols_i[:], pattern=[[1, P]], base=0, channel_multiplier=0).then_inc(consts_ready, 1)
            pool.iota(slot_no_i[:], pattern=[[P, BPAD]], base=0, channel_multiplier=1).then_inc(consts_ready, 1)
            pool.memset(ident[:], 0.0).then_inc(pool_step, 1)
            pool.memset(lmask[:], LORA_SCALE).then_inc(pool_step, 1)
            pool.memset(ones[:], 1.0).then_inc(pool_step, 1)
            pool.memset(tri16[:], 1.0).then_inc(pool_step, 1)
            pool.memset(tri4[:], 1.0).then_inc(pool_step, 1)
            pool.memset(lh_sb[:], 0.0).then_inc(pool_step, 1)
            pool.wait_ge(pool_step, 6)
            pool.affine_select(out=ident[:], in_=ident[:], compare_op=ALU.not_equal, fill=1.0, base=0,
                               pattern=[[-1, P]], channel_multiplier=1).then_inc(consts_ready, 1)
            pool.affine_select(out=lmask[:], in_=lmask[:], compare_op=ALU.is_ge, fill=0.0, base=0,
                               pattern=[[-SEQ_LEN, SEQ_PER_TILE], [0, RANK]],
                               channel_multiplier=1).then_inc(pool_step, 1)
            pool.wait_ge(pool_step, 7)
            pool.affine_select(out=lmask[:], in_=lmask[:], compare_op=ALU.is_ge, fill=0.0, base=SEQ_LEN - 1,
                               pattern=[[SEQ_LEN, SEQ_PER_TILE], [0, RANK]],
                               channel_multiplier=-1).then_inc(consts_ready, 1)
            pool.wait_ge(lora_row_ready, 1)
            for g in range(GROUPS_L):
                pool.indirect_dma_start(lora_sb[:, g, :], None, lora,
                                        bass.IndirectOffsetOnAxis(ap=lora_row[:, g:g + 1], axis=0)).then_inc(lora_in[g], 16)
            pool.affine_select(out=upper[:], in_=ones[:], compare_op=ALU.is_gt, fill=0.0, base=0,
                               pattern=[[1, P]], channel_multiplier=-1).then_inc(consts_ready, 1)
            pool.affine_select(out=tri16[:], in_=tri16[:], compare_op=ALU.is_gt, fill=0.0, base=0,
                               pattern=[[1, E], [-1, E]], channel_multiplier=0).then_inc(consts_ready, 1)
            pool.affine_select(out=tri4[:], in_=tri4[:], compare_op=ALU.is_gt, fill=0.0, base=0,
                               pattern=[[1, GROUPS], [-1, GROUPS]], channel_multiplier=0).then_inc(consts_ready, 1)

            pool.wait_ge(slot_tok_ready, 1)
            for s in range(4):
                pool.wait_ge(xt_stored[s], 16 * TILES // 4)
            def gather(b):
                if b >= 4:
                    pool.wait_ge(xg_turned, b - 3)
                pool.indirect_dma_start(xg_sb[:, b % 4, :], None, xt_rows,
                                        bass.IndirectOffsetOnAxis(ap=slot_tok[:, b:b + 1], axis=0)
                                        ).then_inc(gathered[b % 4], 16)

            def scatter(b):
                pool.wait_ge(y_copied, b + 1)
                pool.indirect_dma_start(y_rows, bass.IndirectOffsetOnAxis(ap=slot_row[:, b:b + 1], axis=0),
                                        y_sb[:, b % 2, :], None).then_inc(y_scattered[b % 2], 16)

            def group(g):
                for b in range(g * UNROLL, (g + 1) * UNROLL):
                    gather(b + UNROLL)
                    scatter(b)

            for b in range(UNROLL):
                gather(b)
            pool.wait_ge(eid_ready, 1)
            top = last_group(pool)
            for g in range(LOOP_END // UNROLL):
                if g * UNROLL < FULL:
                    group(g)
                else:
                    with pool.If(top >= g * UNROLL):
                        group(g)
            for g in range(FULL // UNROLL, LOOP_END // UNROLL + 1):
                with pool.If(top == (g - 1) * UNROLL):
                    for b in range(g * UNROLL, g * UNROLL + DRAINED):
                        scatter(b)

        @block.scalar
        def _(act):
            for g in range(GROUPS_L):
                act.wait_ge(lora_in[g], 16)
            for e in range(0, E, EXPERTS_PER_LOAD):
                n = EXPERTS_PER_LOAD
                act.dma_start(w12_sb[:, e * W12:(e + n) * W12].rearrange("p (e c) -> p e c", e=n),
                              w12[e:e + n].rearrange("e p c -> p e c")).then_inc(experts_in, 16)
                act.dma_start(w3_sb[:, e * DIM:(e + n) * DIM].rearrange("p (e c) -> p e c", e=n),
                              w3[e:e + n].rearrange("e p c -> p e c")).then_inc(experts_in, 16)
            for g in range(GROUPS_L):
                act.wait_ge(loraA_turned, g + 1)
                act.copy(loraA_sb[:, g], bank[2 + g][:].rearrange("p (k r) -> p k r", k=KC)).then_inc(loraA_copied, 1)

            def copy_lhT(i):
                act.wait_ge(lhT_done, i + 1)
                act.copy(lhT_sb[:, i % 2, :], bank[5][:, 0:P]).then_inc(lhT_copied, 1)

            def copy_xtT(i):
                act.wait_ge(xtT_done, i + 1)
                act.copy(xtT_sb[:, :, i * P:(i + 1) * P],
                         bank[2 + i % 2][:].rearrange("p (k t) -> p k t", k=KC)).then_inc(xtT_copied, 1)

            for i in range(TILES):
                copy_lhT(i)
                if i >= 1:
                    copy_xtT(i - 1)
            copy_xtT(TILES - 1)

            act.wait_ge(shifted, 1)
            act.activation(ex[:], lgs[:], ACT.Exp).then_inc(exp_done, 1)
            for u in range(2 * IC):
                act.wait_ge(sh_gate_done, u + 1)
                if u >= 2:
                    act.wait_ge(sh_hidden, u - 1)
                act.activation(sg_sb[:, u % 2, :], bank[2 * (u % 2)][:], ACT.Silu,
                               bias=sb12_sb[:, 0, u % IC:u % IC + 1]).then_inc(sh_silu, 1)
            for n in range(2):
                act.wait_ge(gateT_done, n + 1)
                act.copy(gateT[:, n * 512:(n + 1) * 512], bank[6 + n][0:E + 1, :]).then_inc(gateT_copied, 1)

            def copy_xgT(b, s):
                act.wait_ge(xg_turned, b + 1)
                act.copy(xgT_sb[:, s % 2], bank[s % 2][:].rearrange("p (k t) -> p k t", k=KC)).then_inc(xgT_copied, 1)

            def silu(b, s):
                act.wait_ge(pre_ready, b + 1)
                act.activation(gl_sb[:, s % 2, :], pre_sb[:, s % 2, 0:INTER], ACT.Silu).then_inc(act_ready, 1)

            def copy_hT(b, s):
                act.wait_ge(h_turned, b + 1)
                act.copy(hT_sb[:, s % 2, :], bank[4][:, 0:P]).then_inc(hT_copied, 1)

            def steps(b, s):
                copy_hT(b, s)
                copy_xgT(b + 2, s + 2)
                silu(b + 1, s + 1)

            copy_xgT(0, 0)
            copy_xgT(1, 1)
            silu(0, 0)
            act.wait_ge(eid_ready, 1)
            top = last_group(act)
            with act.Fori(0, LOOP_END, UNROLL) as b:
                with act.If(b < top + UNROLL):
                    for s in range(UNROLL):
                        steps(b + s, s)
            for s in range(DRAINED):
                copy_hT(top + (UNROLL + s), s)
                if s + 2 < DRAINED:
                    copy_xgT(top + (UNROLL + s + 2), s + 2)
                if s + 1 < DRAINED:
                    silu(top + (UNROLL + s + 1), s + 1)

        @block.vector
        def _(dve):
            made = [0]

            def then(ins):
                made[0] += 1
                ins.then_inc(dve_step, 1)
                dve.wait_ge(dve_step, made[0])

            def over_tiles(ap):
                return ap.unsqueeze(1).to_broadcast([P, TILES, E])

            def over_experts(ap):
                return ap.unsqueeze(2).to_broadcast([P, TILES, E])

            dve.wait_ge(consts_ready, 3)
            then(dve.tensor_scalar(part16_i[:], part_i[:], RANK - 1, None, ALU.bitwise_and))
            then(dve.tensor_copy(part16[:], part16_i[:]))
            dve.wait_ge(seq_in, 16)
            then(dve.tensor_copy(slot_f[:], slot_i[:]))
            then(dve.tensor_scalar(slot_f2[:], slot_f[:], float(RANK), None, ALU.mult))
            dve.tensor_scalar(lora_row[:], slot_f2[:], part16[:, 0:1], None, ALU.add).then_inc(lora_row_ready, 1)
            then(dve.tensor_copy(cols[:], cols_i[:]))
            then(dve.tensor_copy(slot_no[:], slot_no_i[:]))
            then(dve.tensor_scalar(thr[:], cols[:, 0:TILES], float(P), None, ALU.mult))
            then(dve.tensor_scalar(desc[:], cols[:, 0:E], -1.0, float(E), ALU.mult, ALU.add))
            dve.memset(gate[:, :, E:E + 1], 1.0).then_inc(consts_f, 1)

            dve.wait_ge(consts_ready, 5)
            dve.wait_ge(small_in, 16 * 6)
            for i in range(TILES):
                dve.wait_ge(lh_done, i + 1)
                c = LR * (i % 2)
                dve.tensor_tensor(lh_sb[:, i % 2, c:c + LR], bank[4][:, 0:LR],
                                  lmask[:].rearrange("p q r -> p (q r)"), ALU.mult).then_inc(lh_masked, 1)
                dve.wait_ge(cond_done, i + 1)
                if i >= 4:
                    dve.wait_ge(xt_stored[i % 4], 16 * (i // 4))
                dve.tensor_tensor(xt_sb[:, i % 4, :], cond_bank(i)[:], condb_sb[:], ALU.add).then_inc(xt_ready, 1)

            def hidden(u):
                dve.wait_ge(sh_up_done, u + 1)
                dve.wait_ge(sh_silu, u + 1)
                n, c = u // IC, u % IC
                dve.scalar_tensor_tensor(out=hsT_sb[:, c, n * HALF:(n + 1) * HALF], in0=bank[2 * (u % 2) + 1][:],
                                         scalar=sb12_sb[:, 1, c:c + 1], in1=sg_sb[:, u % 2, :],
                                         op0=ALU.add, op1=ALU.mult).then_inc(sh_hidden, 1)

            dve.wait_ge(consts_ready, 8)
            dve.wait_ge(logits_done, 1)
            then(dve.tensor_tensor(lg[:], bank[6][:, 0:TILES * E].rearrange("p (i e) -> p i e", e=E),
                                   over_tiles(rb_sb[:]), ALU.add))
            then(dve.tensor_reduce(red[:], lg[:], AX.X, ALU.max))
            dve.tensor_tensor(lgs[:], lg[:], over_experts(red[:]), ALU.subtract).then_inc(shifted, 1)
            dve.wait_ge(exp_done, 1)
            then(dve.tensor_reduce(red[:], ex[:], AX.X, ALU.add))
            then(dve.reciprocal(red2[:], red[:]))
            then(dve.tensor_tensor(tmp[:], ex[:], over_experts(red2[:]), ALU.mult))
            then(dve.tensor_tensor(sc[:], tmp[:], over_tiles(rbias_sb[:]), ALU.add))
            then(dve.tensor_reduce(gmax[:], sc[:].rearrange("p i (g m) -> p i g m", m=PER_GROUP), AX.X, ALU.max))
            pair = [P, TILES, GROUPS, GROUPS]
            mine, other = gmax[:].unsqueeze(3).to_broadcast(pair), gmax[:].unsqueeze(2).to_broadcast(pair)
            then(dve.tensor_tensor(gcmp[:], other, mine, ALU.is_gt))
            then(dve.tensor_tensor(geq[:], other, mine, ALU.is_equal))
            then(dve.tensor_tensor(geq[:], geq[:], tri4[:].unsqueeze(1).to_broadcast(pair), ALU.mult))
            then(dve.tensor_tensor(gcmp[:], gcmp[:], geq[:], ALU.add))
            then(dve.tensor_reduce(gpen[:], gcmp[:], AX.X, ALU.add))
            then(dve.tensor_scalar(gpen[:], gpen[:], float(LIM), -BIG, ALU.is_ge, ALU.mult))
            then(dve.tensor_tensor(sc1[:].rearrange("p i (g m) -> p i g m", m=PER_GROUP),
                                   sc[:].rearrange("p i (g m) -> p i g m", m=PER_GROUP),
                                   gpen[:].unsqueeze(3).to_broadcast([P, TILES, GROUPS, PER_GROUP]), ALU.add))
            for k in range(K):
                then(dve.tensor_reduce(val[:, k, :], sc1[:], AX.X, ALU.max))
                then(dve.tensor_tensor(tmp[:], sc1[:], over_experts(val[:, k, :]), ALU.is_equal))
                then(dve.tensor_tensor(tmp[:], tmp[:], over_tiles(desc[:]), ALU.mult))
                then(dve.tensor_reduce(red[:], tmp[:], AX.X, ALU.max))
                then(dve.tensor_tensor(sel[:, k], over_tiles(desc[:]), over_experts(red[:]), ALU.is_equal))
                if k == 0:
                    then(dve.scalar_tensor_tensor(out=sc1[:], in0=sel[:, 0], scalar=-BIG, in1=sc1[:],
                                                  op0=ALU.mult, op1=ALU.add))
            dve.tensor_tensor(chosen[:], sel[:, 0], sel[:, 1], ALU.add).then_inc(chosen_ready, 1)
            then(dve.tensor_tensor(tmp[:], sel[:, 0], over_experts(val[:, 0, :]), ALU.mult))
            then(dve.tensor_tensor(sc1[:], sel[:, 1], over_experts(val[:, 1, :]), ALU.mult))
            dve.tensor_tensor(gate[:, :, 0:E], tmp[:], sc1[:], ALU.add).then_inc(gate_ready, 1)
            hidden(0)

            dve.wait_ge(cond_done, TILES)
            dve.wait_ge(ranks_done, 1)
            then(dve.tensor_reduce(cnt[:], bank[4][:, P:2 * P].rearrange("p (i e) -> p e i", e=E), AX.X, ALU.add))
            cmp8 = [P, E, TILES]
            then(dve.tensor_tensor(ncmp[:, :, 0:TILES], cnt[:].unsqueeze(2).to_broadcast(cmp8),
                                   thr[:].unsqueeze(1).to_broadcast(cmp8), ALU.is_gt))
            then(dve.tensor_reduce(nblk[:], ncmp[:, :, 0:TILES], AX.X, ALU.add))
            then(dve.tensor_tensor(ncmp[:], nblk[:].unsqueeze(1).to_broadcast([P, E, E]), tri16[:], ALU.mult))
            then(dve.tensor_reduce(base[:], ncmp[:], AX.X, ALU.add))
            then(dve.scalar_tensor_tensor(out=rank[:], in0=over_tiles(base[:]), scalar=float(P),
                                          in1=bank[4][:, 0:P].rearrange("p (i e) -> p i e", e=E),
                                          op0=ALU.mult, op1=ALU.add))
            then(dve.tensor_tensor(selpos, sel[:], rank[:].unsqueeze(1).to_broadcast([P, K, TILES, E]), ALU.mult))
            then(dve.tensor_reduce(pos[:], selpos.rearrange("p k i e -> p (k i) e"), AX.X, ALU.add))
            then(dve.tensor_copy(pos_i[:], pos[:]))
            then(dve.tensor_scalar(off_i[:], pos_i[:], P - 1, None, ALU.bitwise_and))
            then(dve.tensor_scalar(blk_i[:], pos_i[:], P.bit_length() - 1, None, ALU.arith_shift_right))
            then(dve.tensor_copy(off[:], off_i[:]))
            then(dve.tensor_copy(blk[:], blk_i[:]))
            NJ = K * TILES
            then(dve.tensor_scalar(pair_row, slot_no[:, 0:NJ], float(-K * T), None, ALU.add))
            dve.tensor_tensor(onehot_off, off[:].unsqueeze(2).to_broadcast([P, NJ, P]),
                              cols[:].unsqueeze(1).to_broadcast([P, NJ, P]), ALU.is_equal).then_inc(onehots_ready, 1)
            flat = blk_tok.rearrange("p k i b -> p (k i) b")
            then(dve.tensor_tensor(flat, blk[:].unsqueeze(2).to_broadcast([P, NJ, BPAD]),
                                   cols[:, 0:BPAD].unsqueeze(1).to_broadcast([P, NJ, BPAD]), ALU.is_equal))
            dve.tensor_tensor(flat, flat, pair_row.unsqueeze(2).to_broadcast([P, NJ, BPAD]), ALU.mult).then_inc(onehots_ready, 1)
            then(dve.tensor_tensor(ends[:], base[:], nblk[:], ALU.add))
            then(dve.tensor_tensor(ecmp, ends[0:1, :].unsqueeze(1).to_broadcast([1, BPAD, E]),
                                   cols[0:1, 0:BPAD].unsqueeze(2).to_broadcast([1, BPAD, E]), ALU.is_le))
            then(dve.tensor_reduce(eid_f[:], ecmp, AX.X, ALU.add))
            then(dve.tensor_copy(nused[:], ends[0:1, E - 1:E]))
            then(dve.tensor_scalar(nused[:], nused[:], LOOP_END, None, ALU.bitwise_and))
            then(dve.tensor_copy(top_f[:], nused[:]))
            then(dve.tensor_scalar(eid[0:1, BPAD:BPAD + 1], top_f[:], float(UNROLL), None, ALU.subtract))
            then(dve.tensor_scalar(eid[:, 0:BPAD], eid_f[:], float(E - 1), None, ALU.min))
            dve.engine_nop().then_inc(eid_ready, 1)
            hidden(1)
            dve.wait_ge(slots_done, 1)
            then(dve.tensor_scalar(slot_f32, bank[5][:, 0:BPAD], float(K * T), None, ALU.add))
            then(dve.tensor_copy(slot_row[:], slot_f32))
            then(dve.tensor_scalar(slot_tok[:], slot_row[:], T - 1, None, ALU.bitwise_and))
            then(dve.tensor_scalar(slot_empty, slot_f32, float(K * T), None, ALU.is_equal))
            then(dve.tensor_tensor(slot_empty, slot_empty, slot_no[:], ALU.mult))
            dve.tensor_tensor(slot_row[:], slot_f32, slot_empty, ALU.add).then_inc(slot_tok_ready, 1)
            hidden(2)
            hidden(3)

            dve.wait_ge(b12_in, 16)

            def add_bias(b, s):
                e = dve.value_load(eid[0:1, bass.ds(b, 1)], min_val=0, max_val=E - 1)
                dve.wait_ge(a_done, b + 1)
                dve.tensor_tensor(pre_sb[:, s % 2, :], bank[2 + s % 2][:, 0:2 * INTER],
                                  b12_sb[:, bass.ds(e * (2 * INTER), 2 * INTER)], ALU.add).then_inc(pre_ready, 1)

            def times_up(b, s):
                dve.wait_ge(act_ready, b + 1)
                dve.tensor_tensor(h_sb[:, s % 2, :], gl_sb[:, s % 2, :], pre_sb[:, s % 2, INTER:], ALU.mult).then_inc(h_ready, 1)

            def copy_y(b, s):
                dve.wait_ge(y_done, b + 1)
                if not (isinstance(b, int) and b < 2):
                    dve.wait_ge(y_scattered[s % 2], (b - s % 2) * 8)
                dve.tensor_copy(y_sb[:, s % 2, :], bank[5 + s % 2][:]).then_inc(y_copied, 1)

            add_bias(0, 0)
            times_up(0, 0)
            for b in range(UNROLL):
                add_bias(b + 1, b + 1)
                times_up(b + 1, b + 1)
                copy_y(b, b)
            top = last_group(dve)
            with dve.Fori(UNROLL, LOOP_END, UNROLL) as b:
                with dve.If(b < top + UNROLL):
                    for s in range(UNROLL):
                        add_bias(b + (s + 1), s + 1)
                        times_up(b + (s + 1), s + 1)
                        copy_y(b + s, s)
            for s in range(DRAINED):
                if s + 1 < DRAINED:
                    add_bias(top + (UNROLL + s + 1), s + 1)
                    times_up(top + (UNROLL + s + 1), s + 1)
                copy_y(top + (UNROLL + s), s)

            dve.wait_ge(x_in, 16)

            def add_shared(i):
                dve.wait_ge(shared_done, i + 1)
                dve.tensor_tensor(x_sb[:, i, :], x_sb[:, i, :], shared_bank(i)[:], ALU.add).then_inc(acc_shared, 1)

            def add_experts(i):
                dve.wait_ge(y_in[i], 16)
                dve.wait_ge(acc_shared, i + 1)
                for k in range(K):
                    ins = dve.scalar_tensor_tensor(out=x_sb[:, i, :], in0=yg_sb[:, i, k, :],
                                                   scalar=val[:, k, i:i + 1], in1=x_sb[:, i, :],
                                                   op0=ALU.mult, op1=ALU.add)
                    if k < K - 1:
                        then(ins)
                ins.then_inc(acc_done, 1)

            for i in range(TILES):
                add_shared(i)
                if i >= 2:
                    add_experts(i - 2)
            add_experts(TILES - 2)
            add_experts(TILES - 1)

        @block.tensor
        def _(pe):
            def cond_w(i):
                if i % 2 == 0:
                    pe.wait_ge(xT_in[i // 2], 16)
                if i >= 3:
                    pe.wait_ge(xt_ready, i - 2)
                for k in range(KC):
                    pe.matmul(cond_bank(i)[:], xT_sb[:, k, i * P:(i + 1) * P], condW_sb[:, k, :],
                              start=(k == 0), stop=False)

            def lora_h(i):
                g, j = i // 2, i % 2
                if i == 0:
                    pe.wait_ge(loraA_copied, 4)
                for k in range(KC):
                    mm = pe.matmul(bank[4][:, 0:LR], xT_sb[:, k, i * P:(i + 1) * P],
                                   loraA_sb[:, g, k, LR * j:LR * (j + 1)], start=(k == 0), stop=(k == KC - 1))
                mm.then_inc(lh_done, 1)

            def turn_lora_h(i):
                pe.wait_ge(lh_masked, i + 1)
                pe.transpose(bank[5][:, 0:P], lh_sb[:, i % 2, :], ident[:]).then_inc(lhT_done, 1)

            def cond_lora(i):
                pe.wait_ge(lhT_copied, i + 1)
                pe.matmul(cond_bank(i)[:], lhT_sb[:, i % 2, :], lora_sb[:, i // 2, DIM:2 * DIM],
                          start=False, stop=True).then_inc(cond_done, 1)

            def turn_xt(i):
                pe.wait_ge(xt_ready, i + 1)
                if i >= 2:
                    pe.wait_ge(xtT_copied, i - 1)
                for k in range(KC):
                    mm = pe.transpose(bank[2 + i % 2][:, k * P:(k + 1) * P], xt_sb[:, i % 4, k * P:(k + 1) * P], ident[:])
                mm.then_inc(xtT_done, 1)

            def logits(i):
                pe.wait_ge(xtT_copied, i + 1)
                for k in range(KC):
                    mm = pe.matmul(bank[6][:, i * E:(i + 1) * E], xtT_sb[:, k, i * P:(i + 1) * P], rw_sb[:, k, :],
                                   start=(k == 0), stop=(k == KC - 1))
                if i == TILES - 1:
                    mm.then_inc(logits_done, 1)

            pe.wait_ge(condW_in, 16)
            cond_w(0)
            cond_w(1)
            pe.wait_ge(consts_ready, 4)
            for g in range(GROUPS_L):
                pe.wait_ge(lora_in[g], 16)
                for k in range(KC):
                    mm = pe.transpose(bank[2 + g][:, k * P:(k + 1) * P], lora_sb[:, g, k * P:(k + 1) * P], ident[:])
                mm.then_inc(loraA_turned, 1)
            pe.wait_ge(small_in, 16 * 6)
            for i in range(TILES):
                lora_h(i)
                if 1 <= i < TILES - 1:
                    cond_w(i + 1)
                turn_lora_h(i)
                if i >= 2:
                    logits(i - 2)
                if i >= 1:
                    turn_xt(i - 1)
                cond_lora(i)
            turn_xt(TILES - 1)
            logits(TILES - 2)
            logits(TILES - 1)

            def shared_up(u):
                n, c = u // IC, u % IC
                if u >= 2:
                    pe.wait_ge(sh_hidden, u - 1)
                for m, done in ((0, sh_gate_done), (1, sh_up_done)):
                    for k in range(KC):
                        mm = pe.matmul(bank[2 * (u % 2) + m][:], sw12_sb[:, m, k, c * P:(c + 1) * P],
                                       xtT_sb[:, k, n * HALF:(n + 1) * HALF], start=(k == 0), stop=(k == KC - 1))
                    mm.then_inc(done, 1)

            pe.wait_ge(shared_in, 32)
            shared_up(0)
            pe.wait_ge(chosen_ready, 1)
            pe.wait_ge(consts_ready, 8)
            flat = chosen[:].rearrange("p i e -> p (i e)")
            pe.matmul(bank[4][:, 0:P], upper[:], flat, start=True, stop=False)
            for i in range(TILES - 1):
                n = TILES - 1 - i
                pe.matmul(bank[4][:, (i + 1) * E:P], ones[:], chosen[:, i, :].unsqueeze(1).to_broadcast([P, n, E]),
                          start=False, stop=(i == TILES - 2))
            pe.matmul(bank[4][:, P:2 * P], ones[:], flat, start=True, stop=True).then_inc(ranks_done, 1)
            shared_up(1)
            shared_up(2)
            pe.wait_ge(onehots_ready, 2)
            for j in range(K * TILES):
                mm = pe.matmul(bank[5][:, 0:BPAD], onehot_off[:, j, :], blk_tok[:, j // TILES, j % TILES, :],
                               start=(j == 0), stop=(j == K * TILES - 1))
            mm.then_inc(slots_done, 1)
            pe.wait_ge(consts_f, 1)
            pe.wait_ge(gate_ready, 1)
            for i in range(TILES):
                mm = pe.transpose(bank[6 + i // 4][0:E + 1, (i % 4) * P:(i % 4 + 1) * P], gate[:, i, :], ident[:])
                if i % 4 == 3:
                    mm.then_inc(gateT_done, 1)
            shared_up(3)

            def turn_xg(b, s):
                pe.wait_ge(gathered[s % 4], ((b - s % 4) + 4) * 4)
                for k in range(KC):
                    mm = pe.transpose(bank[s % 2][:, k * P:(k + 1) * P], xg_sb[:, s % 4, k * P:(k + 1) * P], ident[:])
                mm.then_inc(xg_turned, 1)

            def expert_of(b):
                return pe.value_load(eid[0:1, bass.ds(b, 1)], min_val=0, max_val=E - 1)

            def up(b, s, e, first, last):
                if first == 0:
                    pe.wait_ge(xgT_copied, b + 1)
                for k in range(first, last):
                    mm = pe.matmul(bank[2 + s % 2][:, 0:2 * INTER], xgT_sb[:, s % 2, k, :],
                                   w12_sb[:, bass.ds(e * W12 + k * 2 * INTER, 2 * INTER)],
                                   start=(k == 0), stop=(k == KC - 1))
                if last == KC:
                    mm.then_inc(a_done, 1)

            def turn_h(b, s):
                pe.wait_ge(h_ready, b + 1)
                pe.transpose(bank[4][:, 0:P], h_sb[:, s % 2, :], ident[:]).then_inc(h_turned, 1)

            def down(b, s):
                e = expert_of(b)
                pe.wait_ge(hT_copied, b + 1)
                if not (isinstance(b, int) and b < 2):
                    pe.wait_ge(y_copied, b - 1)
                pe.matmul(bank[5 + s % 2][:], hT_sb[:, s % 2, :], w3_sb[:, bass.ds(e * DIM, DIM)],
                          start=True, stop=True).then_inc(y_done, 1)

            def steps(b, s):
                e = expert_of(b + 1)
                up(b + 1, s + 1, e, 0, KC // 2)
                turn_h(b, s)
                turn_xg(b + 2, s + 2)
                up(b + 1, s + 1, e, KC // 2, KC)
                down(b, s)

            pe.wait_ge(sh_hidden, 4)
            pe.wait_ge(slot_tok_ready, 1)
            pe.wait_ge(gateT_copied, 2)
            pe.wait_ge(eid_ready, 1)
            turn_xg(0, 0)
            turn_xg(1, 1)
            pe.wait_ge(experts_in, 16 * 2 * E // EXPERTS_PER_LOAD)
            up(0, 0, expert_of(0), 0, KC)
            for b in range(UNROLL):
                steps(b, b)
            top = last_group(pe)
            with pe.Fori(UNROLL, LOOP_END, UNROLL) as b:
                with pe.If(b < top + UNROLL):
                    for s in range(UNROLL):
                        steps(b + s, s)
            for s in range(DRAINED):
                b = top + (UNROLL + s)
                if s + 1 < DRAINED:
                    e = expert_of(b + 1)
                    up(b + 1, s + 1, e, 0, KC // 2)
                turn_h(b, s)
                if s + 2 < DRAINED:
                    turn_xg(b + 2, s + 2)
                if s + 1 < DRAINED:
                    up(b + 1, s + 1, e, KC // 2, KC)
                down(b, s)

            for i in range(TILES):
                if i >= 4:
                    pe.wait_ge(acc_shared, i - 3)
                for c in range(IC):
                    pe.matmul(shared_bank(i)[:], hsT_sb[:, c, i * P:(i + 1) * P], sw3_sb[:, c, :],
                              start=(c == 0), stop=False)
                pe.matmul(shared_bank(i)[:], gateT[:, i * P:(i + 1) * P], b3s_sb[:], start=False, stop=True
                          ).then_inc(shared_done, 1)


def kernel(x, itok_B_0_23, L0_cond_W, L0_cond_b, L0_cond_lora_As, L0_cond_lora_Bs, L0_ffn_router_w,
           L0_ffn_router_b, L0_ffn_router_bias, L0_ffn_ew1, L0_ffn_eb1, L0_ffn_ew2, L0_ffn_eb2, L0_ffn_ew3,
           L0_ffn_eb3, L0_ffn_sw1, L0_ffn_sb1, L0_ffn_sw2, L0_ffn_sb2, L0_ffn_sw3, L0_ffn_sb3):
    import numpy as np
    import concourse.bacc as bacc
    from concourse.bass_utils import run_bass_kernel_spmd

    def chunks(w):
        w = np.asarray(w)
        return w.reshape(-1, P, w.shape[-1]).transpose(1, 0, 2)

    xf = np.asarray(x).reshape(T, DIM)
    w12 = np.concatenate([np.asarray(L0_ffn_ew1), np.asarray(L0_ffn_ew2)], axis=-1)
    w12 = w12.reshape(E, KC, P, 2 * INTER).transpose(0, 2, 1, 3).reshape(E, P, W12)
    laid = {
        "x": xf,
        "xT": xf.T.reshape(KC, P, T),
        "seq_slot": np.repeat(np.asarray(itok_B_0_23), RANK).reshape(GROUPS_L, P).T,
        "condWT": np.asarray(L0_cond_W).T.reshape(KC, P, DIM),
        "cond_b": np.asarray(L0_cond_b),
        "lora": np.concatenate([np.asarray(L0_cond_lora_As).transpose(0, 2, 1),
                                np.asarray(L0_cond_lora_Bs)], axis=-1).reshape(SLOTS * RANK, 2 * DIM),
        "router_w": chunks(L0_ffn_router_w),
        "router_b": np.asarray(L0_ffn_router_b),
        "router_bias": np.asarray(L0_ffn_router_bias),
        "w12": w12,
        "b12": np.concatenate([np.asarray(L0_ffn_eb1), np.asarray(L0_ffn_eb2)], axis=-1).reshape(-1),
        "w3": np.asarray(L0_ffn_ew3),
        "b3s": np.concatenate([np.asarray(L0_ffn_eb3), np.asarray(L0_ffn_sb3)[None]], axis=0),
        "sw12": np.stack([chunks(L0_ffn_sw1), chunks(L0_ffn_sw2)], axis=1),
        "sb12": np.stack([np.asarray(L0_ffn_sb1).reshape(IC, P).T, np.asarray(L0_ffn_sb2).reshape(IC, P).T], axis=1),
        "sw3": chunks(L0_ffn_sw3),
    }
    nc = bacc.Bacc("TRN2", target_bir_lowering=False, num_devices=1)
    arrays, args = {}, []
    for name, a in laid.items():
        a = np.ascontiguousarray(a)
        arrays[f"in_{name}"] = a
        args.append(nc.dram_tensor(f"in_{name}", a.shape, mybir.dt.from_np(a.dtype), kind="ExternalInput").ap())
    args.append(nc.dram_tensor("out_0", (T, DIM), F32, kind="ExternalOutput").ap())
    program(nc, *args)
    r = run_bass_kernel_spmd(nc, [arrays], core_ids=[0])
    return r.results[0]["out_0"].reshape(SEQS, SEQ_LEN, DIM)
```

```python
from contextlib import ExitStack

import concourse.bass as bass
from concourse import mybir

F32 = mybir.dt.float32
F32R = mybir.dt.float32r
I32 = mybir.dt.int32
ALU = mybir.AluOpType
ACT = mybir.ActivationFunctionType
AX = mybir.AxisListType

P = 128
SEQS, SEQ_LEN, DIM = 32, 32, 512
T = SEQS * SEQ_LEN
TILES = T // P
KC = DIM // P
SLOTS, RANK = 32, 16
LORA_SCALE = 32 / RANK
SEQ_PER_GROUP = P // RANK
GROUPS_L = SEQS * RANK // P
GT = T // GROUPS_L
E, INTER, SHARED = 16, 128, 256
GROUPS, PER_GROUP, LIM, K = 4, 4, 2, 2
BLOCKS = (K * T + E * (P - 1)) // P
FULL = K * T // P
BPAD = 32
W12 = KC * 2 * INTER
IC = SHARED // P
HALF = T // 2
XCHUNKS = GROUPS_L + 1
WARM_UP = 16
SHARED_OUT = TILES - 1
BIG = 3.0e38
UNROLL = 4
XT_RING = 4
EXPERTS_PER_LOAD = 4
ARENA_KIB = 180
LOOP_END = BLOCKS - BLOCKS % UNROLL
DRAINED = BLOCKS - LOOP_END
LOOP_AT, LEFT_AT, EVEN_AT, ODD_AT = range(BPAD, BPAD + 4)
assert E // 2 == TILES == 2 * GROUPS_L
assert LOOP_END == 28 and DRAINED == UNROLL - 1 == 3 and FULL % UNROLL == 0


def program(nc, x, xT, seq_slot, condWT, cond_b, lora, router_w, router_b, router_bias,
            w12, b12, w3, b3s, sw12, sb12, sw3, out):
    xt_rows = nc.dram_tensor("xt_rows", (T, DIM), F32, kind="Internal").ap()
    y_rows = nc.dram_tensor("y_rows", (K * T + BLOCKS * P, DIM), F32, kind="Internal").ap()

    with ExitStack() as ctx:
        def sb(name, shape, dt=F32):
            return ctx.enter_context(nc.sbuf_tensor(name, shape, dt))

        def sem(name):
            return ctx.enter_context(nc.semaphore(name))

        bank = [ctx.enter_context(nc.psum_tensor(f"bank{i}", [P, 512], F32)) for i in range(8)]

        rw_raw = sb("rw_raw", [P, KC, E])
        rw_split = sb("rw_split", [P, KC, 2, E], F32R)
        b3s_sb = sb("b3s_sb", [E + 1, DIM])
        condb_sb = sb("condb_sb", [P, DIM])
        rb_sb = sb("rb_sb", [P, E])
        rbias_sb = sb("rbias_sb", [P, E])
        sb12_sb = sb("sb12_sb", [P, 2, IC])
        lhT_sb = sb("lhT_sb", [P, GT])
        lhT_split = sb("lhT_h", [P, GT], F32R), sb("lhT_l", [P, GT], F32R)

        arena_at = nc.sbuf_base
        sb("arena", [P, ARENA_KIB * 256])

        def at(kib, name, shape, dt=F32):
            return nc.alloc_sbuf_tensor_at(name, shape, dt, offset=arena_at + kib * 1024)

        xT_split = [(at(32 + 8 * g, f"xT_h{g}", [P, KC, GT], F32R), at(36 + 8 * g, f"xT_l{g}", [P, KC, GT], F32R))
                    for g in range(GROUPS_L)]
        w12_sb = at(0, "w12_sb", [P, E * W12])
        yg_sb = at(0, "yg_sb", [P, TILES, K, DIM])
        condW_split = at(64, "condW_h", [P, KC, DIM], F32R), at(72, "condW_l", [P, KC, DIM], F32R)
        xT_raw = at(80, "xT_raw", [P, 2, KC, GT])
        condW_raw = at(88, "condW_raw", [P, KC, DIM])
        sw12_raw = at(88, "sw12_raw", [P, 2, KC, SHARED])
        w3_sb = at(64, "w3_sb", [P, E * DIM])
        xtT_split = [(at(96, "xtT_h0", [P, KC, HALF], F32R), at(104, "xtT_l0", [P, KC, HALF], F32R)),
                     (at(112, "xtT_h1", [P, KC, HALF], F32R), at(120, "xtT_l1", [P, KC, HALF], F32R))]
        b12_sb = at(96, "b12_sb", [P, E * 2 * INTER])
        x_sb = at(112, "x_sb", [P, TILES, DIM])
        sw12_split = at(128, "sw12_h", [P, 2, KC, SHARED], F32R), at(136, "sw12_l", [P, 2, KC, SHARED], F32R)
        xgT_sb = at(128, "xgT_sb", [P, 2, KC, P])
        y_sb = at(132, "y_sb", [P, 2, DIM])
        pre_sb = at(136, "pre_sb", [P, 2, 2 * INTER])
        gl_sb = at(138, "gl_sb", [P, 2, INTER])
        h_sb = at(139, "h_sb", [P, 2, INTER])
        hT_sb = at(140, "hT_sb", [P, 2, P])
        sw3_raw = at(144, "sw3_raw", [P, IC, DIM])
        sw3_split = at(148, "sw3_h", [P, IC, DIM], F32R), at(144, "sw3_l", [P, IC, DIM], F32R)
        xt_ring = at(148, "xt_ring01", [P, 2, DIM]), at(176, "xt_ring23", [P, 2, DIM])
        lora_raw = at(152, "lora_raw", [P, 2, 2 * DIM])
        loraA_split = at(160, "loraA_h", [P, 2, KC, P], F32R), at(164, "loraA_l", [P, 2, KC, P], F32R)
        loraB_split = at(168, "loraB_h", [P, 2, DIM], F32R), at(172, "loraB_l", [P, 2, DIM], F32R)
        onehot_off = at(152, "onehot_off", [P, K * TILES, P], F32R)
        hsT_sb = at(160, "hsT_sb", [P, IC, T])
        hsT_split = at(152, "hsT_h", [P, IC, T], F32R), at(160, "hsT_l", [P, IC, T], F32R)
        blk_tok = at(168, "blk_tok", [P, K * TILES, BPAD], F32R)
        blk_hit = at(172, "blk_hit", [P, K * TILES, BPAD])
        selpos = at(170, "selpos", [P, K, TILES, E])
        xg_sb = at(168, "xg_sb", [P, 4, DIM])
        sg_sb = at(176, "sg_sb", [P, 2, HALF])

        ident = sb("ident", [P, P])
        ones = sb("ones", [P, P])
        upper_r = sb("upper_r", [P, P], F32R)
        ones_r = sb("ones_r", [P, P], F32R)
        lmask = sb("lmask", [P, SEQ_PER_GROUP, SEQ_LEN])
        tri16 = sb("tri16", [P, E, E])
        tri4 = sb("tri4", [P, GROUPS, GROUPS])
        cols_i = sb("cols_i", [P, P], I32)
        cols = sb("cols", [P, P])
        part_i = sb("part_i", [P, 1], I32)
        part16_i = sb("part16_i", [P, 1], I32)
        part16 = sb("part16", [P, 1])
        slot_no_i = sb("slot_no_i", [P, BPAD], I32)
        thr = sb("thr", [P, TILES])
        desc = sb("desc", [P, E])

        slot_i = sb("slot_i", [P, GROUPS_L], I32)
        slot_f = sb("slot_f", [P, GROUPS_L])
        slot_f2 = sb("slot_f2", [P, GROUPS_L])
        lora_row = sb("lora_row", [P, GROUPS_L], I32)
        lg = sb("lg", [P, TILES, E])
        lgs = sb("lgs", [P, TILES, E])
        ex = sb("ex", [P, TILES, E])
        sc = sb("sc", [P, TILES, E])
        sc1 = sb("sc1", [P, TILES, E])
        tmp = sb("tmp", [P, TILES, E])
        red = sb("red", [P, TILES])
        red2 = sb("red2", [P, TILES])
        gmax = sb("gmax", [P, TILES, GROUPS])
        gcmp = sb("gcmp", [P, TILES, GROUPS, GROUPS])
        geq = sb("geq", [P, TILES, GROUPS, GROUPS])
        gpen = sb("gpen", [P, TILES, GROUPS])
        sel = sb("sel", [P, K, TILES, E])
        val = sb("val", [P, K, TILES])
        chosen = sb("chosen", [P, TILES, E], F32R)
        gate = sb("gate", [P, TILES, E + 1])
        gateT = sb("gateT", [E + 1, T])
        cnt = sb("cnt", [P, E])
        ncmp = sb("ncmp", [P, E, E])
        nblk = sb("nblk", [P, E])
        base = sb("base", [P, E])
        ends = sb("ends", [P, E])
        ecmp = condb_sb[0:1, :].rearrange("p (b e) -> p b e", e=E)
        eid_f = sb("eid_f", [1, BPAD])
        top_f = sb("top_f", [1, 1])
        nused = sb("nused", [1, 1], I32)
        ngroups = sb("ngroups", [1, 1], I32)
        nused_even = sb("nused_even", [1, 1], I32)
        even16 = sb("even16", [1, 1])
        eid = sb("eid", [1, BPAD + 4], I32)
        rows_stored = sem("rows_stored")
        rank = lgs
        pos = sb("pos", [P, K * TILES])
        pos_i = sb("pos_i", [P, K * TILES], I32)
        off_i = sb("off_i", [P, K * TILES], I32)
        blk_i = sb("blk_i", [P, K * TILES], I32)
        spent = ex[:].rearrange("p i e -> p (i e)")
        slot_f32, slot_empty, pair_row = spent[:, 0:BPAD], spent[:, BPAD:2 * BPAD], spent[:, 2 * BPAD:2 * BPAD + K * TILES]
        slot_pair = sb("slot_pair", [P, BPAD], I32)
        slot_tok = sb("slot_tok", [P, BPAD], I32)
        slot_row = sb("slot_row", [P, BPAD], I32)
        slot_no = sb("slot_no", [P, BPAD])

        seq_in, small_in, x_in, b12_in, sw3_in = (
            sem("seq_in"), sem("small_in"), sem("x_in"), sem("b12_in"), sem("sw3_in"))
        condW_in = [sem(f"condW_in{k}") for k in range(KC)]
        xT_in = [sem(f"xT_in{c}") for c in range(XCHUNKS)]
        sw12_in, experts_in = sem("sw12_in"), sem("experts_in")
        lora_in = [sem(f"lora_in{g}") for g in range(GROUPS_L)]
        condW_hi, condW_done, rw_hi, rw_done = sem("condW_hi"), sem("condW_done"), sem("rw_hi"), sem("rw_done")
        xT_hi, xT_done, sw12_hi, sw12_done = sem("xT_hi"), sem("xT_done"), sem("sw12_hi"), sem("sw12_done")
        loraA_hi, loraA_done, loraB_hi, loraB_done = (
            sem("loraA_hi"), sem("loraA_done"), sem("loraB_hi"), sem("loraB_done"))
        lhT_hi, lhT_done, xtT_hi, xtT_done = sem("lhT_hi"), sem("lhT_done"), sem("xtT_hi"), sem("xtT_done")
        pool_step, consts_ready, consts_f = sem("pool_step"), sem("consts_ready"), sem("consts_f")
        lora_row_ready = sem("lora_row_ready")
        loraA_turned, lh_done, lh_masked = sem("loraA_turned"), sem("lh_done"), sem("lh_masked")
        cond_done, xt_ready, xt_turned = sem("cond_done"), sem("xt_ready"), sem("xt_turned")
        xt_stored = [sem(f"xt_stored{s}") for s in range(XT_RING)]
        logits_done, shifted, exp_done, dve_step = sem("logits_done"), sem("shifted"), sem("exp_done"), sem("dve_step")
        chosen_ready, ranks_done, onehots_ready, slots_done = (
            sem("chosen_ready"), sem("ranks_done"), sem("onehots_ready"), sem("slots_done"))
        hs_hi, hs_done, sw3_hi, sw3_done = sem("hs_hi"), sem("hs_done"), sem("sw3_hi"), sem("sw3_done")
        ahead_read, scaled, pair_added = sem("ahead_read"), sem("scaled"), sem("pair_added")
        left_ready, blk_hit_ready, blk_tok_ready, slot_row_ready = (
            sem("left_ready"), sem("blk_hit_ready"), sem("blk_tok_ready"), sem("slot_row_ready"))
        slot_tok_ready, eid_ready, gate_ready, gateT_done, gateT_copied = (
            sem("slot_tok_ready"), sem("eid_ready"), sem("gate_ready"), sem("gateT_done"), sem("gateT_copied"))
        sh_gate_done, sh_up_done, sh_silu, sh_hidden = (
            sem("sh_gate_done"), sem("sh_up_done"), sem("sh_silu"), sem("sh_hidden"))
        gathered = [sem(f"gathered{s}") for s in range(4)]
        xg_turned, xgT_copied, a_done, pre_ready, act_ready, h_ready = (
            sem("xg_turned"), sem("xgT_copied"), sem("a_done"), sem("pre_ready"), sem("act_ready"), sem("h_ready"))
        h_turned, hT_copied, y_done, y_copied = sem("h_turned"), sem("hT_copied"), sem("y_done"), sem("y_copied")
        y_scattered = [sem(f"y_scattered{s}") for s in range(2)]
        shared_done, acc_shared, y_in = sem("shared_done"), sem("acc_shared"), [sem(f"y_in{i}") for i in range(TILES)]
        acc_done, out_stored = sem("acc_done"), sem("out_stored")

        def xt_place(i):
            return xt_ring[i % XT_RING // 2][:, i % 2, :]

        def cond_bank(i):
            return bank[(0, 1, 7)[i % 3]]

        def hidden_bank(u, m):
            return bank[((7, 0), (2, 3), (1, 5), (7, 0))[u][m]]

        def shared_bank(i):
            return bank[(7, 0, 1, 2)[i % 4]]

        def last_group(eng):
            return eng.value_load(eid[0:1, LOOP_AT:LOOP_AT + 1], min_val=FULL - UNROLL, max_val=LOOP_END - UNROLL)

        def blocks_left(eng):
            return eng.value_load(eid[0:1, LEFT_AT:LEFT_AT + 1], min_val=0, max_val=DRAINED)

        def each_group(eng, first, top, group):
            with eng.Fori(first, FULL, UNROLL) as b:
                group(b)
            with eng.If(top >= FULL):
                with eng.Fori(FULL, LOOP_END, UNROLL) as b:
                    with eng.If(b < top + UNROLL):
                        group(b)

        def drained(eng, drain):
            left = blocks_left(eng)
            for n in range(1, DRAINED + 1):
                with eng.If(left == n):
                    drain(n)

        def load_experts(eng, first, last, w_sb, w):
            n, width = min(EXPERTS_PER_LOAD, last - first), w.shape[-1]
            for e in range(first, last, n):
                eng.dma_start(w_sb[:, e * width:(e + n) * width].rearrange("p (e c) -> p e c", e=n),
                              w[e:e + n].rearrange("e p c -> p e c")).then_inc(experts_in, 16)

        def xT_chunk(c):
            return (0, slice(c * P, (c + 1) * P)) if c < 2 else (c - 1, slice(0, GT))

        out_order = [*range(TILES - 2), TILES - 1, TILES - 2]

        block = ctx.enter_context(nc.Block())

        @block.sync
        def _(sp):
            sp.dma_start(slot_i[:], seq_slot).then_inc(seq_in, 16)
            def load_xT(c):
                g, tokens = xT_chunk(c)
                if c >= 3:
                    sp.wait_ge(xT_done, c - 1)
                sp.dma_start(xT_raw[:, g % 2, :, tokens],
                             xT.rearrange("k p (g t) -> g p k t", g=GROUPS_L)[g][:, :, tokens]).then_inc(xT_in[c], 16)

            sp.dma_start(condW_raw[:, 0, :], condWT[0]).then_inc(condW_in[0], 16)
            load_xT(0)
            for k in range(1, KC):
                sp.dma_start(condW_raw[:, k, :], condWT[k]).then_inc(condW_in[k], 16)
            load_xT(1)
            load_xT(2)
            sp.dma_start(condb_sb[:], cond_b.partition_broadcast(P)).then_inc(small_in, 16)
            sp.dma_start(rw_raw[:], router_w).then_inc(small_in, 16)
            sp.dma_start(rb_sb[:], router_b.partition_broadcast(P)).then_inc(small_in, 16)
            sp.dma_start(rbias_sb[:], router_bias.partition_broadcast(P)).then_inc(small_in, 16)
            sp.dma_start(sb12_sb[:], sb12).then_inc(small_in, 16)
            sp.dma_start(b3s_sb[:], b3s).then_inc(small_in, 16)
            load_xT(3)
            load_xT(4)
            sp.wait_ge(condW_done, KC)
            sp.dma_start(sw12_raw[:], sw12).then_inc(sw12_in, 16)
            sp.dma_start(sw3_raw[:], sw3).then_inc(sw3_in, 16)
            for i in range(TILES):
                sp.wait_ge(xt_ready, i + 1)
                sp.dma_start(xt_rows[i * P:(i + 1) * P, :], xt_place(i)).then_inc(xt_stored[i % XT_RING], 16)
                if i % 2 == 1:
                    sp.wait_ge(cond_done, i + 1)
                    load_experts(sp, E // 2 + i - 1, E // 2 + i + 1, w12_sb, w12)
            sp.wait_ge(sw12_done, 2)
            sp.wait_ge(xT_done, XCHUNKS)
            load_experts(sp, 0, E, w3_sb, w3)
            sp.wait_ge(sh_up_done, IC)
            sp.dma_start(b12_sb[:], b12.partition_broadcast(P)).then_inc(b12_in, 16)
            sp.wait_ge(sh_up_done, 2 * IC)
            for i in range(TILES):
                sp.wait_ge(y_copied, UNROLL + i)
                sp.dma_start(x_sb[:, i, :], x[i * P:(i + 1) * P, :]).then_inc(x_in, 16)
            sp.wait_ge(slot_row_ready, 1)
            even = sp.value_load(eid[0:1, EVEN_AT:EVEN_AT + 1], min_val=16 * FULL // 2, max_val=16 * (BLOCKS + 1) // 2)
            odd = sp.value_load(eid[0:1, ODD_AT:ODD_AT + 1], min_val=16 * FULL // 2, max_val=16 * BLOCKS // 2)
            sp.wait_ge(y_scattered[0], even)
            sp.sem_inc(rows_stored, 1)
            sp.wait_ge(y_scattered[1], odd)
            sp.sem_inc(rows_stored, 1)
            sp.wait_ge(rows_stored, 2)
            for i in range(TILES):
                sp.dma_start(yg_sb[:, i], y_rows[0:K * T, :].rearrange("(k i p) d -> i p k d", k=K, p=P)[i]
                             ).then_inc(y_in[i], 16)
            for n in range(TILES):
                i = out_order[n]
                sp.wait_ge(acc_done, n + 1)
                sp.dma_start(out[i * P:(i + 1) * P, :], x_sb[:, i, :]).then_inc(out_stored, 16)
            sp.wait_ge(out_stored, 16 * TILES)

        @block.gpsimd
        def _(pool):
            pool.iota(part_i[:], pattern=[[0, 1]], base=0, channel_multiplier=1).then_inc(consts_ready, 1)
            pool.iota(cols_i[:], pattern=[[1, P]], base=0, channel_multiplier=0).then_inc(consts_ready, 1)
            pool.iota(slot_no_i[:], pattern=[[P, BPAD]], base=0, channel_multiplier=1).then_inc(consts_ready, 1)
            pool.memset(ident[:], 0.0).then_inc(pool_step, 1)
            pool.memset(lmask[:], LORA_SCALE).then_inc(pool_step, 1)
            pool.memset(ones[:], 1.0).then_inc(pool_step, 1)
            pool.memset(tri16[:], 1.0).then_inc(pool_step, 1)
            pool.memset(tri4[:], 1.0).then_inc(pool_step, 1)
            pool.wait_ge(pool_step, 5)
            pool.affine_select(out=ident[:], in_=ident[:], compare_op=ALU.not_equal, fill=1.0, base=0,
                               pattern=[[-1, P]], channel_multiplier=1).then_inc(consts_ready, 1)
            pool.affine_select(out=lmask[:], in_=lmask[:], compare_op=ALU.is_ge, fill=0.0, base=0,
                               pattern=[[-RANK, SEQ_PER_GROUP], [0, SEQ_LEN]],
                               channel_multiplier=1).then_inc(pool_step, 1)
            pool.wait_ge(pool_step, 6)
            pool.affine_select(out=lmask[:], in_=lmask[:], compare_op=ALU.is_ge, fill=0.0, base=RANK - 1,
                               pattern=[[RANK, SEQ_PER_GROUP], [0, SEQ_LEN]],
                               channel_multiplier=-1).then_inc(consts_ready, 1)
            def gather_lora(g):
                if g >= 2:
                    pool.wait_ge(loraA_turned, g - 1)
                    pool.wait_ge(loraB_done, g - 1)
                pool.indirect_dma_start(lora_raw[:, g % 2, :], None, lora,
                                        bass.IndirectOffsetOnAxis(ap=lora_row[:, g:g + 1], axis=0)).then_inc(lora_in[g], 16)

            pool.wait_ge(lora_row_ready, 1)
            gather_lora(0)
            gather_lora(1)
            pool.affine_select(out=upper_r[:], in_=ones[:], compare_op=ALU.is_gt, fill=0.0, base=0,
                               pattern=[[1, P]], channel_multiplier=-1).then_inc(consts_ready, 1)
            pool.tensor_copy(ones_r[:], ones[:]).then_inc(consts_ready, 1)
            pool.affine_select(out=tri16[:], in_=tri16[:], compare_op=ALU.is_gt, fill=0.0, base=0,
                               pattern=[[1, E], [-1, E]], channel_multiplier=0).then_inc(consts_ready, 1)
            pool.affine_select(out=tri4[:], in_=tri4[:], compare_op=ALU.is_gt, fill=0.0, base=0,
                               pattern=[[1, GROUPS], [-1, GROUPS]], channel_multiplier=0).then_inc(consts_ready, 1)

            gather_lora(2)
            gather_lora(3)

            by_block = [P, K * TILES, BPAD]
            pool.wait_ge(blk_hit_ready, 1)
            pool.tensor_tensor(blk_tok[:], blk_hit[:], pair_row.unsqueeze(2).to_broadcast(by_block), ALU.mult
                               ).then_inc(blk_tok_ready, 1)

            pool.wait_ge(slot_tok_ready, 1)
            for s in range(XT_RING):
                pool.wait_ge(xt_stored[s], 16 * TILES // XT_RING)
            def gather(b):
                if b >= 4:
                    pool.wait_ge(xg_turned, b - 3)
                pool.indirect_dma_start(xg_sb[:, b % 4, :], None, xt_rows,
                                        bass.IndirectOffsetOnAxis(ap=slot_tok[:, b:b + 1], axis=0)
                                        ).then_inc(gathered[b % 4], 16)

            def scatter(b):
                pool.wait_ge(y_copied, b + 1)
                pool.indirect_dma_start(y_rows, bass.IndirectOffsetOnAxis(ap=slot_row[:, b:b + 1], axis=0),
                                        y_sb[:, b % 2, :], None).then_inc(y_scattered[b % 2], 16)

            def group(g):
                for b in range(g * UNROLL, (g + 1) * UNROLL):
                    gather(b + UNROLL)
                    scatter(b)

            for b in range(UNROLL):
                gather(b)
            pool.wait_ge(slot_row_ready, 1)
            pool.wait_ge(eid_ready, 1)
            top = last_group(pool)
            for g in range(LOOP_END // UNROLL):
                if g * UNROLL < FULL:
                    group(g)
                else:
                    with pool.If(top >= g * UNROLL):
                        group(g)
            left = blocks_left(pool)
            for g in range(FULL // UNROLL, LOOP_END // UNROLL + 1):
                with pool.If(top == (g - 1) * UNROLL):
                    for n in range(DRAINED):
                        with pool.If(left > n):
                            scatter(g * UNROLL + n)
            for i in range(SHARED_OUT):
                pool.wait_ge(scaled, K * (i + 1))
                pool.tensor_tensor(yg_sb[:, i, 0, :], yg_sb[:, i, 0, :], yg_sb[:, i, 1, :], ALU.add).then_inc(pair_added, 1)

        @block.scalar
        def _(act):
            def hi_xT(c):
                g, tokens = xT_chunk(c)
                act.wait_ge(xT_in[c], 16)
                act.copy(xT_split[g][0][:, :, tokens], xT_raw[:, g % 2, :, tokens]).then_inc(xT_hi, 1)

            def hi_condW(k):
                act.wait_ge(condW_in[k], 16)
                act.copy(condW_split[0][:, k, :], condW_raw[:, k, :]).then_inc(condW_hi, 1)

            def hi_lora(g):
                act.wait_ge(loraA_turned, g + 1)
                if g >= 2:
                    act.wait_ge(lh_done, g - 1)
                act.copy(loraA_split[0][:, g % 2], bank[5][:].rearrange("p (k r) -> p k r", k=KC)).then_inc(loraA_hi, 1)
                if g >= 2:
                    act.wait_ge(cond_done, 2 * g - 2)
                act.copy(loraB_split[0][:, g % 2], lora_raw[:, g % 2, DIM:2 * DIM]).then_inc(loraB_hi, 1)

            def hi_lhT(g):
                act.wait_ge(lh_masked, g + 1)
                if g >= 1:
                    act.wait_ge(cond_done, 2 * g)
                act.copy(lhT_split[0][:], lhT_sb[:]).then_inc(lhT_hi, 1)

            def hi_xtT(i):
                act.wait_ge(xt_turned, i + 1)
                n, t = i * P // HALF, i * P % HALF
                act.copy(xtT_split[n][0][:, :, t:t + P],
                         bank[2 + i % 2][:].rearrange("p (k t) -> p k t", k=KC)).then_inc(xtT_hi, 1)

            hi_condW(0)
            hi_xT(0)
            for k in range(1, KC):
                hi_condW(k)
            hi_xT(1)
            hi_xT(2)
            hi_lora(0)
            hi_lhT(0)
            for i in range(TILES):
                g = i // 2 + 1
                if i % 2 == 0 and g < GROUPS_L:
                    hi_lora(g)
                if i % 2 == 1 and g < GROUPS_L:
                    hi_lhT(g)
                hi_xtT(i)
                if i % 2 == 0 and g + 2 < XCHUNKS:
                    hi_xT(g + 2)
                if i == 1:
                    load_experts(act, 0, E // 2, w12_sb, w12)
                if i in (3, 4):
                    if i == 3:
                        act.wait_ge(sw12_in, 16)
                    act.copy(sw12_split[0][:, i - 3], sw12_raw[:, i - 3]).then_inc(sw12_hi, 1)

            act.wait_ge(shifted, 1)
            act.activation(ex[:], lgs[:], ACT.Exp).then_inc(exp_done, 1)
            for s in range(2, XT_RING):
                act.wait_ge(xt_stored[s], 16 * TILES // XT_RING)
            for u in range(2 * IC):
                act.wait_ge(sh_gate_done, u + 1)
                if u >= 2:
                    act.wait_ge(sh_hidden, u - 1)
                act.activation(sg_sb[:, u % 2, :], hidden_bank(u, 0)[:], ACT.Silu,
                               bias=sb12_sb[:, 0, u % IC:u % IC + 1]).then_inc(sh_silu, 1)

            def hi_hs(u):
                act.wait_ge(sh_hidden, u + 1)
                n, c = u // IC, u % IC
                act.copy(hsT_split[0][:, c, n * HALF:(n + 1) * HALF], hsT_sb[:, c, n * HALF:(n + 1) * HALF]).then_inc(hs_hi, 1)

            act.wait_ge(slots_done, 1)
            hi_hs(0)
            hi_hs(1)
            for s in range(2):
                act.wait_ge(xt_stored[s], 16 * TILES // XT_RING)
            act.wait_ge(sw3_in, 16)
            act.copy(sw3_split[0][:], sw3_raw[:]).then_inc(sw3_hi, 1)
            hi_hs(2)
            hi_hs(3)
            for n in range(2):
                act.wait_ge(gateT_done, n + 1)
                act.copy(gateT[:, n * 512:(n + 1) * 512], bank[(4, 2)[n]][0:E + 1, :]).then_inc(gateT_copied, 1)

            def copy_xgT(b, s):
                act.wait_ge(xg_turned, b + 1)
                act.copy(xgT_sb[:, s % 2], bank[s % 2][:].rearrange("p (k t) -> p k t", k=KC)).then_inc(xgT_copied, 1)

            def silu(b, s):
                act.wait_ge(pre_ready, b + 1)
                act.activation(gl_sb[:, s % 2, :], pre_sb[:, s % 2, 0:INTER], ACT.Silu).then_inc(act_ready, 1)

            def copy_hT(b, s):
                act.wait_ge(h_turned, b + 1)
                act.copy(hT_sb[:, s % 2, :], bank[4][:, 0:P]).then_inc(hT_copied, 1)

            def steps(b, s):
                copy_hT(b, s)
                copy_xgT(b + 2, s + 2)
                silu(b + 1, s + 1)

            copy_xgT(0, 0)
            copy_xgT(1, 1)
            silu(0, 0)
            act.wait_ge(eid_ready, 1)
            top = last_group(act)

            def group(b):
                for s in range(UNROLL):
                    steps(b + s, s)

            def drain(n):
                for s in range(n):
                    copy_hT(top + (UNROLL + s), s)
                    if s + 2 < n:
                        copy_xgT(top + (UNROLL + s + 2), s + 2)
                    if s + 1 < n:
                        silu(top + (UNROLL + s + 1), s + 1)

            each_group(act, 0, top, group)
            drained(act, drain)

            for i in range(SHARED_OUT):
                act.wait_ge(y_in[i], 16)
                for k in range(K):
                    act.activation(yg_sb[:, i, k, :], yg_sb[:, i, k, :], ACT.Copy, scale=val[:, k, i:i + 1]
                                   ).then_inc(scaled, 1)

        @block.vector
        def _(dve):
            made = [0]

            def then(ins):
                made[0] += 1
                ins.then_inc(dve_step, 1)
                dve.wait_ge(dve_step, made[0])

            def over_tiles(ap):
                return ap.unsqueeze(1).to_broadcast([P, TILES, E])

            def over_experts(ap):
                return ap.unsqueeze(2).to_broadcast([P, TILES, E])

            dve.wait_ge(consts_ready, 3)
            then(dve.tensor_scalar(part16_i[:], part_i[:], RANK - 1, None, ALU.bitwise_and))
            then(dve.tensor_copy(part16[:], part16_i[:]))
            dve.wait_ge(seq_in, 16)
            then(dve.tensor_copy(slot_f[:], slot_i[:]))
            then(dve.tensor_scalar(slot_f2[:], slot_f[:], float(RANK), None, ALU.mult))
            dve.tensor_scalar(lora_row[:], slot_f2[:], part16[:, 0:1], None, ALU.add).then_inc(lora_row_ready, 1)
            then(dve.tensor_copy(cols[:], cols_i[:]))
            then(dve.tensor_copy(slot_no[:], slot_no_i[:]))
            then(dve.tensor_scalar(thr[:], cols[:, 0:TILES], float(P), None, ALU.mult))
            then(dve.tensor_scalar(desc[:], cols[:, 0:E], -1.0, float(E), ALU.mult, ALU.add))
            dve.memset(gate[:, :, E:E + 1], 1.0).then_inc(consts_f, 1)

            def rest(lo, whole, hi, made_sem):
                dve.tensor_tensor(lo, whole, hi.bitcast(F32), ALU.subtract).then_inc(made_sem, 1)

            def lo_condW(k):
                dve.wait_ge(condW_hi, k + 1)
                rest(condW_split[1][:, k, :], condW_raw[:, k, :], condW_split[0][:, k, :], condW_done)

            def lo_xT(c):
                g, tokens = xT_chunk(c)
                hi, lo = xT_split[g]
                dve.wait_ge(xT_hi, c + 1)
                rest(lo[:, :, tokens], xT_raw[:, g % 2, :, tokens], hi[:, :, tokens], xT_done)

            def lo_lora(g):
                dve.wait_ge(loraA_hi, g + 1)
                rest(loraA_split[1][:, g % 2], bank[5][:].rearrange("p (k r) -> p k r", k=KC),
                     loraA_split[0][:, g % 2], loraA_done)
                dve.wait_ge(loraB_hi, g + 1)
                rest(loraB_split[1][:, g % 2], lora_raw[:, g % 2, DIM:2 * DIM], loraB_split[0][:, g % 2], loraB_done)

            def mask_lh(g):
                dve.wait_ge(lh_done, g + 1)
                dve.tensor_tensor(lhT_sb[:], bank[4][:, 0:GT], lmask[:].rearrange("p q r -> p (q r)"), ALU.mult
                                  ).then_inc(lh_masked, 1)
                dve.wait_ge(lhT_hi, g + 1)
                rest(lhT_split[1][:], lhT_sb[:], lhT_split[0][:], lhT_done)

            def lo_xtT(i):
                dve.wait_ge(xtT_hi, i + 1)
                n, t = i * P // HALF, i * P % HALF
                rest(xtT_split[n][1][:, :, t:t + P], bank[2 + i % 2][:].rearrange("p (k t) -> p k t", k=KC),
                     xtT_split[n][0][:, :, t:t + P], xtT_done)

            lo_condW(0)
            lo_xT(0)
            for k in range(1, KC):
                lo_condW(k)
            lo_xT(1)
            lo_xT(2)
            lo_lora(0)
            dve.wait_ge(consts_ready, 5)
            mask_lh(0)
            dve.wait_ge(small_in, 16 * 6)
            dve.tensor_copy(rw_split[:, :, 0, :], rw_raw[:]).then_inc(rw_hi, 1)
            dve.wait_ge(rw_hi, 1)
            rest(rw_split[:, :, 1, :], rw_raw[:], rw_split[:, :, 0, :], rw_done)
            for i in range(TILES):
                dve.wait_ge(cond_done, i + 1)
                if i >= XT_RING:
                    dve.wait_ge(xt_stored[i % XT_RING], 16 * (i // XT_RING))
                dve.tensor_tensor(xt_place(i), cond_bank(i)[:], condb_sb[:], ALU.add).then_inc(xt_ready, 1)
                g = i // 2 + 1
                if i % 2 == 0 and g < GROUPS_L:
                    lo_lora(g)
                if i % 2 == 1 and g < GROUPS_L:
                    mask_lh(g)
                lo_xtT(i)
                if i % 2 == 0 and g + 2 < XCHUNKS:
                    lo_xT(g + 2)
                if i in (3, 4):
                    dve.wait_ge(sw12_hi, i - 2)
                    rest(sw12_split[1][:, i - 3], sw12_raw[:, i - 3], sw12_split[0][:, i - 3], sw12_done)

            def hidden(u):
                dve.wait_ge(sh_up_done, u + 1)
                dve.wait_ge(sh_silu, u + 1)
                n, c = u // IC, u % IC
                dve.scalar_tensor_tensor(out=hsT_sb[:, c, n * HALF:(n + 1) * HALF], in0=hidden_bank(u, 1)[:],
                                         scalar=sb12_sb[:, 1, c:c + 1], in1=sg_sb[:, u % 2, :],
                                         op0=ALU.add, op1=ALU.mult).then_inc(sh_hidden, 1)

            dve.wait_ge(consts_ready, 9)
            dve.wait_ge(logits_done, 1)
            parts = bank[6][:, 0:TILES * 2 * E].rearrange("p (i m e) -> p i m e", m=2, e=E)
            then(dve.tensor_tensor(lg[:], parts[:, :, 0, :], over_tiles(rb_sb[:]), ALU.add))
            then(dve.tensor_tensor(lg[:], parts[:, :, 1, :], lg[:], ALU.add))
            then(dve.tensor_reduce(red[:], lg[:], AX.X, ALU.max))
            dve.tensor_tensor(lgs[:], lg[:], over_experts(red[:]), ALU.subtract).then_inc(shifted, 1)
            dve.wait_ge(exp_done, 1)
            then(dve.tensor_reduce(red[:], ex[:], AX.X, ALU.add))
            then(dve.reciprocal(red2[:], red[:]))
            then(dve.tensor_tensor(tmp[:], ex[:], over_experts(red2[:]), ALU.mult))
            then(dve.tensor_tensor(sc[:], tmp[:], over_tiles(rbias_sb[:]), ALU.add))
            then(dve.tensor_reduce(gmax[:], sc[:].rearrange("p i (g m) -> p i g m", m=PER_GROUP), AX.X, ALU.max))
            pair = [P, TILES, GROUPS, GROUPS]
            mine, other = gmax[:].unsqueeze(3).to_broadcast(pair), gmax[:].unsqueeze(2).to_broadcast(pair)
            then(dve.tensor_tensor(gcmp[:], other, mine, ALU.is_gt))
            then(dve.tensor_tensor(geq[:], other, mine, ALU.is_equal))
            then(dve.tensor_tensor(geq[:], geq[:], tri4[:].unsqueeze(1).to_broadcast(pair), ALU.mult))
            then(dve.tensor_tensor(gcmp[:], gcmp[:], geq[:], ALU.add))
            then(dve.tensor_reduce(gpen[:], gcmp[:], AX.X, ALU.add))
            then(dve.tensor_scalar(gpen[:], gpen[:], float(LIM), -BIG, ALU.is_ge, ALU.mult))
            then(dve.tensor_tensor(sc1[:].rearrange("p i (g m) -> p i g m", m=PER_GROUP),
                                   sc[:].rearrange("p i (g m) -> p i g m", m=PER_GROUP),
                                   gpen[:].unsqueeze(3).to_broadcast([P, TILES, GROUPS, PER_GROUP]), ALU.add))
            for k in range(K):
                then(dve.tensor_reduce(val[:, k, :], sc1[:], AX.X, ALU.max))
                then(dve.tensor_tensor(tmp[:], sc1[:], over_experts(val[:, k, :]), ALU.is_equal))
                then(dve.tensor_tensor(tmp[:], tmp[:], over_tiles(desc[:]), ALU.mult))
                then(dve.tensor_reduce(red[:], tmp[:], AX.X, ALU.max))
                then(dve.tensor_tensor(sel[:, k], over_tiles(desc[:]), over_experts(red[:]), ALU.is_equal))
                if k == 0:
                    then(dve.scalar_tensor_tensor(out=sc1[:], in0=sel[:, 0], scalar=-BIG, in1=sc1[:],
                                                  op0=ALU.mult, op1=ALU.add))
            dve.tensor_tensor(chosen[:], sel[:, 0], sel[:, 1], ALU.add).then_inc(chosen_ready, 1)
            then(dve.tensor_scalar(pair_row, slot_no[:, 0:K * TILES], float(-K * T), None, ALU.add))
            hidden(0)
            hidden(1)
            dve.wait_ge(ranks_done, 1)
            then(dve.tensor_reduce(cnt[:], bank[4][:, P:2 * P].rearrange("p (i e) -> p e i", e=E), AX.X, ALU.add))
            cmp8 = [P, E, TILES]
            then(dve.tensor_tensor(ncmp[:, :, 0:TILES], cnt[:].unsqueeze(2).to_broadcast(cmp8),
                                   thr[:].unsqueeze(1).to_broadcast(cmp8), ALU.is_gt))
            then(dve.tensor_reduce(nblk[:], ncmp[:, :, 0:TILES], AX.X, ALU.add))
            then(dve.tensor_tensor(ncmp[:], nblk[:].unsqueeze(1).to_broadcast([P, E, E]), tri16[:], ALU.mult))
            then(dve.tensor_reduce(base[:], ncmp[:], AX.X, ALU.add))
            then(dve.scalar_tensor_tensor(out=rank[:], in0=over_tiles(base[:]), scalar=float(P),
                                          in1=bank[4][:, 0:P].rearrange("p (i e) -> p i e", e=E),
                                          op0=ALU.mult, op1=ALU.add))
            then(dve.tensor_tensor(selpos[:], sel[:], rank[:].unsqueeze(1).to_broadcast([P, K, TILES, E]), ALU.mult))
            then(dve.tensor_reduce(pos[:], selpos[:].rearrange("p k i e -> p (k i) e"), AX.X, ALU.add))
            then(dve.tensor_copy(pos_i[:], pos[:]))
            then(dve.tensor_scalar(blk_i[:], pos_i[:], P.bit_length() - 1, None, ALU.arith_shift_right))
            then(dve.tensor_scalar(off_i[:], pos_i[:], P - 1, None, ALU.bitwise_and))
            NJ = K * TILES
            dve.tensor_tensor(blk_hit[:], blk_i[:].unsqueeze(2).to_broadcast([P, NJ, BPAD]),
                              cols_i[:, 0:BPAD].unsqueeze(1).to_broadcast([P, NJ, BPAD]), ALU.is_equal).then_inc(blk_hit_ready, 1)
            for j in range(0, NJ, NJ // 2):
                by_offset = [P, NJ // 2, P]
                dve.tensor_tensor(onehot_off[:, j:j + NJ // 2], off_i[:, j:j + NJ // 2].unsqueeze(2).to_broadcast(by_offset),
                                  cols_i[:].unsqueeze(1).to_broadcast(by_offset), ALU.is_equal).then_inc(onehots_ready, 1)
            then(dve.tensor_tensor(tmp[:], sel[:, 0], over_experts(val[:, 0, :]), ALU.mult))
            then(dve.tensor_tensor(sc1[:], sel[:, 1], over_experts(val[:, 1, :]), ALU.mult))
            dve.tensor_tensor(gate[:, :, 0:E], tmp[:], sc1[:], ALU.add).then_inc(gate_ready, 1)
            dve.wait_ge(slots_done, 1)
            then(dve.tensor_copy(slot_pair[:], bank[6][:, 0:BPAD]))
            dve.tensor_scalar(slot_tok[:], slot_pair[:], T - 1, None, ALU.bitwise_and).then_inc(slot_tok_ready, 1)
            hidden(2)
            hidden(3)
            then(dve.tensor_tensor(ends[:], base[:], nblk[:], ALU.add))
            then(dve.tensor_tensor(ecmp, ends[0:1, :].unsqueeze(1).to_broadcast([1, BPAD, E]),
                                   cols[0:1, 0:BPAD].unsqueeze(2).to_broadcast([1, BPAD, E]), ALU.is_le))
            then(dve.tensor_reduce(eid_f[:], ecmp, AX.X, ALU.add))
            then(dve.tensor_copy(nused[:], ends[0:1, E - 1:E]))
            dve.tensor_scalar(eid[0:1, LEFT_AT:LEFT_AT + 1], nused[:], DRAINED, None, ALU.bitwise_and).then_inc(left_ready, 1)
            then(dve.tensor_scalar(ngroups[:], nused[:], LOOP_END, None, ALU.bitwise_and))
            then(dve.tensor_copy(top_f[:], ngroups[:]))
            then(dve.tensor_scalar(eid[0:1, LOOP_AT:LOOP_AT + 1], top_f[:], float(UNROLL), None, ALU.subtract))
            then(dve.tensor_scalar(eid[:, 0:BPAD], eid_f[:], float(E - 1), None, ALU.min))
            dve.wait_ge(left_ready, 1)
            dve.engine_nop().then_inc(eid_ready, 1)
            then(dve.tensor_scalar(slot_f32, slot_pair[:], float(K * T), None, ALU.add))
            then(dve.tensor_scalar(slot_empty, slot_pair[:], 0.0, None, ALU.is_equal))
            then(dve.tensor_tensor(slot_empty, slot_empty, slot_no[:], ALU.mult))
            then(dve.tensor_tensor(slot_row[:], slot_f32, slot_empty, ALU.add))
            then(dve.tensor_scalar(nused_even[:], nused[:], -2, None, ALU.bitwise_and))
            then(dve.tensor_copy(even16[:], nused_even[:]))
            then(dve.tensor_scalar(even16[:], even16[:], 8.0, None, ALU.mult))
            then(dve.tensor_copy(eid[0:1, ODD_AT:ODD_AT + 1], even16[:]))
            dve.scalar_tensor_tensor(out=eid[0:1, EVEN_AT:EVEN_AT + 1], in0=ends[0:1, E - 1:E], scalar=16.0,
                                     in1=even16[:], op0=ALU.mult, op1=ALU.subtract).then_inc(slot_row_ready, 1)

            dve.wait_ge(b12_in, 16)

            def add_bias(b, s):
                e = dve.value_load(eid[0:1, bass.ds(b, 1)], min_val=0, max_val=E - 1)
                dve.wait_ge(a_done, b + 1)
                dve.tensor_tensor(pre_sb[:, s % 2, :], bank[2 + s % 2][:, 0:2 * INTER],
                                  b12_sb[:, bass.ds(e * (2 * INTER), 2 * INTER)], ALU.add).then_inc(pre_ready, 1)

            def times_up(b, s):
                dve.wait_ge(act_ready, b + 1)
                dve.tensor_tensor(h_sb[:, s % 2, :], gl_sb[:, s % 2, :], pre_sb[:, s % 2, INTER:], ALU.mult).then_inc(h_ready, 1)

            def copy_y(b, s):
                dve.wait_ge(y_done, b + 1)
                if not (isinstance(b, int) and b < 2):
                    dve.wait_ge(y_scattered[s % 2], (b - s % 2) * 8)
                dve.tensor_copy(y_sb[:, s % 2, :], bank[5 + s % 2][:]).then_inc(y_copied, 1)

            add_bias(0, 0)
            times_up(0, 0)
            for b in range(UNROLL):
                add_bias(b + 1, b + 1)
                times_up(b + 1, b + 1)
                copy_y(b, b)
                dve.wait_ge(hs_hi, b + 1)
                n, c = b // IC, b % IC
                unit = (slice(None), c, slice(n * HALF, (n + 1) * HALF))
                rest(hsT_split[1][unit], hsT_sb[unit], hsT_split[0][unit], hs_done)
                if b < IC:
                    dve.wait_ge(sw3_hi, 1)
                    rest(sw3_split[1][:, b, :], sw3_raw[:, b, :], sw3_split[0][:, b, :], sw3_done)
            top = last_group(dve)

            def group(b):
                for s in range(UNROLL):
                    add_bias(b + (s + 1), s + 1)
                    times_up(b + (s + 1), s + 1)
                    copy_y(b + s, s)

            def drain(n):
                for s in range(n):
                    if s + 1 < n:
                        add_bias(top + (UNROLL + s + 1), s + 1)
                        times_up(top + (UNROLL + s + 1), s + 1)
                    copy_y(top + (UNROLL + s), s)

            each_group(dve, UNROLL, top, group)
            drained(dve, drain)

            dve.wait_ge(x_in, 16 * TILES)

            def add_shared(i):
                dve.wait_ge(shared_done, i + 1)
                dve.tensor_tensor(x_sb[:, i, :], x_sb[:, i, :], shared_bank(i)[:], ALU.add).then_inc(acc_shared, 1)

            def add_experts(i):
                if i < SHARED_OUT:
                    dve.wait_ge(pair_added, i + 1)
                    dve.wait_ge(acc_shared, i + 1)
                    dve.tensor_tensor(x_sb[:, i, :], x_sb[:, i, :], yg_sb[:, i, 0, :], ALU.add).then_inc(acc_done, 1)
                    return
                dve.wait_ge(y_in[i], 16)
                dve.wait_ge(acc_shared, i + 1)
                for k in range(K):
                    ins = dve.scalar_tensor_tensor(out=x_sb[:, i, :], in0=yg_sb[:, i, k, :],
                                                   scalar=val[:, k, i:i + 1], in1=x_sb[:, i, :],
                                                   op0=ALU.mult, op1=ALU.add)
                    if k < K - 1:
                        then(ins)
                ins.then_inc(acc_done, 1)

            for i in range(TILES):
                add_shared(i)
                if i == TILES - 4:
                    add_experts(0)
                if i == TILES - 3:
                    add_experts(1)
                    add_experts(2)
                if i == TILES - 2:
                    add_experts(3)
                    add_experts(4)
            add_experts(5)
            for i in reversed(range(TILES - 2, TILES)):
                add_experts(i)

        @block.tensor
        def _(pe):
            def product(out, a, b, start, stop):
                for n, (p, q) in enumerate(((0, 0), (0, 1), (1, 0))):
                    mm = pe.matmul(out, a[p], b[q], start=(start and n == 0), stop=(stop and n == 2))
                return mm

            def xT_tile(k, i):
                return [part[:, k, i % 2 * P:(i % 2 + 1) * P] for part in xT_split[i // 2]]

            def cond_w(i, first, last):
                if first == 0:
                    pe.wait_ge(xT_done, i + 1 if i < 2 else i // 2 + 2)
                    if i >= 3:
                        pe.wait_ge(xt_ready, i - 2)
                for k in range(first, last):
                    if i == 0:
                        pe.wait_ge(condW_done, k + 1)
                    product(cond_bank(i)[:], xT_tile(k, i), [part[:, k, :] for part in condW_split],
                            start=(k == 0), stop=False)

            def turn_lora(g):
                pe.wait_ge(lora_in[g], 16)
                for k in range(KC):
                    mm = pe.transpose(bank[5][:, k * P:(k + 1) * P], lora_raw[:, g % 2, k * P:(k + 1) * P], ident[:])
                mm.then_inc(loraA_turned, 1)

            def lora_h(g):
                pe.wait_ge(loraA_done, g + 1)
                pe.wait_ge(xT_done, g + 2)
                for k in range(KC):
                    mm = product(bank[4][:, 0:GT], [part[:, g % 2, k, :] for part in loraA_split],
                                 [part[:, k, :] for part in xT_split[g]],
                                 start=(k == 0), stop=(k == KC - 1))
                mm.then_inc(lh_done, 1)

            def cond_lora(i):
                t = i % 2 * P
                if i % 2 == 0:
                    pe.wait_ge(lhT_done, i // 2 + 1)
                    pe.wait_ge(loraB_done, i // 2 + 1)
                product(cond_bank(i)[:], [part[:, t:t + P] for part in lhT_split],
                        [part[:, i // 2 % 2, :] for part in loraB_split], start=False, stop=True).then_inc(cond_done, 1)

            def turn_xt(i):
                pe.wait_ge(xt_ready, i + 1)
                if i >= 2:
                    pe.wait_ge(xtT_done, i - 1)
                for k in range(KC):
                    mm = pe.transpose(bank[2 + i % 2][:, k * P:(k + 1) * P], xt_place(i)[:, k * P:(k + 1) * P], ident[:])
                mm.then_inc(xt_turned, 1)

            def logits(i):
                pe.wait_ge(xtT_done, i + 1)
                n, t = i * P // HALF, i * P % HALF
                hi, lo = xtT_split[n]
                for k in range(KC):
                    pe.matmul(bank[6][:, 2 * i * E:2 * (i + 1) * E], hi[:, k, t:t + P],
                              rw_split[:, k].rearrange("p m e -> p (m e)"), start=(k == 0), stop=False)
                    mm = pe.matmul(bank[6][:, 2 * i * E:(2 * i + 1) * E], lo[:, k, t:t + P],
                                   rw_split[:, k, 0, :], start=False, stop=(k == KC - 1))
                if i == TILES - 1:
                    mm.then_inc(logits_done, 1)

            def shared_up(u, parts=(0, 1), first=0, last=KC):
                n, c = u // IC, u % IC
                if u == 3 and first == 0 and parts[0] == 0:
                    pe.wait_ge(sh_hidden, 1)
                for m in parts:
                    for k in range(first, last):
                        mm = product(hidden_bank(u, m)[:], [part[:, m, k, c * P:(c + 1) * P] for part in sw12_split],
                                     [part[:, k, :] for part in xtT_split[n]], start=(k == 0), stop=(k == KC - 1))
                    if last == KC:
                        mm.then_inc((sh_gate_done, sh_up_done)[m], 1)

            pe.wait_ge(consts_ready, 4)
            for _ in range(WARM_UP):
                pe.transpose(bank[7][:, 0:P], ident[:], ident[:])
            cond_w(0, 0, KC)
            cond_w(1, 0, KC)
            turn_lora(0)
            cond_w(2, 0, KC // 2)
            lora_h(0)
            for i in range(TILES):
                g = i // 2 + 1
                if i == 0:
                    cond_w(2, KC // 2, KC)
                cond_lora(i)
                if 0 < i < TILES - 2:
                    cond_w(i + 2, KC // 2, KC)
                if i == TILES - 2:
                    pe.wait_ge(sw12_done, 2)
                if i >= TILES - 2:
                    shared_up(0, (0,), (i - TILES + 2) * KC // 2, (i - TILES + 3) * KC // 2)
                if i % 2 == 0 and g < GROUPS_L:
                    turn_lora(g)
                if i % 2 == 1 and g < GROUPS_L:
                    lora_h(g)
                turn_xt(i)
                if i + 3 < TILES:
                    cond_w(i + 3, 0, KC // 2)
                if i == 1:
                    pe.wait_ge(rw_done, 1)
                if i >= 1:
                    logits(i - 1)
            shared_up(0, (1,), 0, KC // 2)
            logits(TILES - 1)
            shared_up(0, (1,), KC // 2, KC)
            shared_up(1)
            shared_up(2, (0,))
            pe.wait_ge(chosen_ready, 1)
            pe.wait_ge(consts_ready, 9)
            flat = chosen[:].rearrange("p i e -> p (i e)")
            pe.matmul(bank[4][:, 0:P], upper_r[:], flat, start=True, stop=False)
            for i in range(TILES - 1):
                n = TILES - 1 - i
                pe.matmul(bank[4][:, (i + 1) * E:P], ones_r[:], chosen[:, i, :].unsqueeze(1).to_broadcast([P, n, E]),
                          start=False, stop=(i == TILES - 2))
            pe.matmul(bank[4][:, P:2 * P], ones_r[:], flat, start=True, stop=True).then_inc(ranks_done, 1)
            shared_up(2, (1,))
            shared_up(3, (0,))
            shared_up(3, (1,), 0, KC // 2)
            pe.wait_ge(blk_tok_ready, 1)
            for j in range(K * TILES):
                if j % TILES == 0:
                    pe.wait_ge(onehots_ready, j // TILES + 1)
                mm = pe.matmul(bank[6][:, 0:BPAD], onehot_off[:, j, :], blk_tok[:, j, :],
                               start=(j == 0), stop=(j == K * TILES - 1))
            mm.then_inc(slots_done, 1)
            shared_up(3, (1,), KC // 2, KC)
            pe.wait_ge(consts_f, 1)
            pe.wait_ge(gate_ready, 1)
            pe.wait_ge(sh_hidden, 2)
            for i in range(TILES):
                mm = pe.transpose(bank[(4, 2)[i // 4]][0:E + 1, (i % 4) * P:(i % 4 + 1) * P], gate[:, i, :], ident[:])
                if i % 4 == 3:
                    mm.then_inc(gateT_done, 1)

            def turn_xg(b, s):
                pe.wait_ge(gathered[s % 4], ((b - s % 4) + 4) * 4)
                for k in range(KC):
                    mm = pe.transpose(bank[s % 2][:, k * P:(k + 1) * P], xg_sb[:, s % 4, k * P:(k + 1) * P], ident[:])
                mm.then_inc(xg_turned, 1)

            def expert_of(b):
                return pe.value_load(eid[0:1, bass.ds(b, 1)], min_val=0, max_val=E - 1)

            def up(b, s, e, first, last):
                if first == 0:
                    pe.wait_ge(xgT_copied, b + 1)
                for k in range(first, last):
                    mm = pe.matmul(bank[2 + s % 2][:, 0:2 * INTER], xgT_sb[:, s % 2, k, :],
                                   w12_sb[:, bass.ds(e * W12 + k * 2 * INTER, 2 * INTER)],
                                   start=(k == 0), stop=(k == KC - 1))
                if last == KC:
                    mm.then_inc(a_done, 1)

            def turn_h(b, s):
                pe.wait_ge(h_ready, b + 1)
                pe.transpose(bank[4][:, 0:P], h_sb[:, s % 2, :], ident[:]).then_inc(h_turned, 1)

            def down(b, s):
                e = expert_of(b)
                pe.wait_ge(hT_copied, b + 1)
                if not (isinstance(b, int) and b < 2):
                    pe.wait_ge(y_copied, b - 1)
                pe.matmul(bank[5 + s % 2][:], hT_sb[:, s % 2, :], w3_sb[:, bass.ds(e * DIM, DIM)],
                          start=True, stop=True).then_inc(y_done, 1)

            def steps(b, s):
                e = expert_of(b + 1)
                up(b + 1, s + 1, e, 0, KC // 2)
                turn_h(b, s)
                turn_xg(b + 2, s + 2)
                up(b + 1, s + 1, e, KC // 2, KC)
                down(b, s)

            pe.wait_ge(sh_hidden, 4)
            pe.wait_ge(slot_tok_ready, 1)
            pe.wait_ge(gateT_copied, 2)
            turn_xg(0, 0)
            turn_xg(1, 1)
            pe.wait_ge(eid_ready, 1)
            pe.wait_ge(experts_in, 16 * ((E + E // 2) // EXPERTS_PER_LOAD + E // 2 // 2))
            up(0, 0, expert_of(0), 0, KC)
            for b in range(UNROLL):
                steps(b, b)
            top = last_group(pe)

            def group(b):
                for s in range(UNROLL):
                    steps(b + s, s)

            def drain(n):
                for s in range(n):
                    b = top + (UNROLL + s)
                    if s + 1 < n:
                        e = expert_of(b + 1)
                        up(b + 1, s + 1, e, 0, KC // 2)
                    turn_h(b, s)
                    if s + 2 < n:
                        turn_xg(b + 2, s + 2)
                    if s + 1 < n:
                        up(b + 1, s + 1, e, KC // 2, KC)
                    down(b, s)

            each_group(pe, UNROLL, top, group)
            drained(pe, drain)

            pe.wait_ge(xgT_copied, top + (UNROLL + 2))
            pe.sem_inc(ahead_read, 1)
            pe.wait_ge(pre_ready, top + (UNROLL + 1))
            pe.sem_inc(ahead_read, 1)
            pe.wait_ge(ahead_read, 2)
            pe.wait_ge(sw3_done, IC)
            pe.wait_ge(hs_done, 2 * IC)
            for i in range(TILES):
                if i >= 4:
                    pe.wait_ge(acc_shared, i - 3)
                for c in range(IC):
                    product(shared_bank(i)[:], [part[:, c, i * P:(i + 1) * P] for part in hsT_split],
                            [part[:, c, :] for part in sw3_split], start=(c == 0), stop=False)
                pe.matmul(shared_bank(i)[:], gateT[:, i * P:(i + 1) * P], b3s_sb[:], start=False, stop=True
                          ).then_inc(shared_done, 1)


def kernel(x, itok_B_0_23, L0_cond_W, L0_cond_b, L0_cond_lora_As, L0_cond_lora_Bs, L0_ffn_router_w,
           L0_ffn_router_b, L0_ffn_router_bias, L0_ffn_ew1, L0_ffn_eb1, L0_ffn_ew2, L0_ffn_eb2, L0_ffn_ew3,
           L0_ffn_eb3, L0_ffn_sw1, L0_ffn_sb1, L0_ffn_sw2, L0_ffn_sb2, L0_ffn_sw3, L0_ffn_sb3):
    import numpy as np
    import concourse.bacc as bacc
    from concourse.bass_utils import run_bass_kernel_spmd

    def chunks(w):
        w = np.asarray(w)
        return w.reshape(-1, P, w.shape[-1]).transpose(1, 0, 2)

    xf = np.asarray(x).reshape(T, DIM)
    w12 = np.concatenate([np.asarray(L0_ffn_ew1), np.asarray(L0_ffn_ew2)], axis=-1)
    w12 = w12.reshape(E, KC, P, 2 * INTER).transpose(0, 2, 1, 3).reshape(E, P, W12)
    laid = {
        "x": xf,
        "xT": xf.T.reshape(KC, P, T),
        "seq_slot": np.repeat(np.asarray(itok_B_0_23), RANK).reshape(GROUPS_L, P).T,
        "condWT": np.asarray(L0_cond_W).T.reshape(KC, P, DIM),
        "cond_b": np.asarray(L0_cond_b),
        "lora": np.concatenate([np.asarray(L0_cond_lora_As).transpose(0, 2, 1),
                                np.asarray(L0_cond_lora_Bs)], axis=-1).reshape(SLOTS * RANK, 2 * DIM),
        "router_w": chunks(L0_ffn_router_w),
        "router_b": np.asarray(L0_ffn_router_b),
        "router_bias": np.asarray(L0_ffn_router_bias),
        "w12": w12,
        "b12": np.concatenate([np.asarray(L0_ffn_eb1), np.asarray(L0_ffn_eb2)], axis=-1).reshape(-1),
        "w3": np.asarray(L0_ffn_ew3),
        "b3s": np.concatenate([np.asarray(L0_ffn_eb3), np.asarray(L0_ffn_sb3)[None]], axis=0),
        "sw12": np.stack([chunks(L0_ffn_sw1), chunks(L0_ffn_sw2)], axis=1),
        "sb12": np.stack([np.asarray(L0_ffn_sb1).reshape(IC, P).T, np.asarray(L0_ffn_sb2).reshape(IC, P).T], axis=1),
        "sw3": chunks(L0_ffn_sw3),
    }
    nc = bacc.Bacc("TRN2", target_bir_lowering=False, num_devices=1)
    arrays, args = {}, []
    for name, a in laid.items():
        a = np.ascontiguousarray(a)
        arrays[f"in_{name}"] = a
        args.append(nc.dram_tensor(f"in_{name}", a.shape, mybir.dt.from_np(a.dtype), kind="ExternalInput").ap())
    args.append(nc.dram_tensor("out_0", (T, DIM), F32, kind="ExternalOutput").ap())
    program(nc, *args)
    r = run_bass_kernel_spmd(nc, [arrays], core_ids=[0])
    return r.results[0]["out_0"].reshape(SEQS, SEQ_LEN, DIM)
```
